# Optimizing a Trainium2 kernel written in Bass

```python
import numpy as np
import jax
import jax.numpy as jnp

def _softmax(x, axis=-1):
    return jax.nn.softmax(x, axis=axis)

def _gelu(x):
    return jax.nn.gelu(x, approximate=True)

def _silu(x):
    return jax.nn.silu(x)

def _sigmoid(x):
    return jax.nn.sigmoid(x)

def _layernorm(x, axis=-1, eps=1e-05):
    m = jnp.mean(x, axis=axis, keepdims=True)
    v = jnp.var(x, axis=axis, keepdims=True)
    return (x - m) / jnp.sqrt(v + eps)

def _scatter_add(tgt, idx, src, axis=0):
    return tgt.at[idx].add(src)

def _segment_sum(src, seg, n):
    return jax.ops.segment_sum(src, seg, n)
kernel_name = 'mk_dlrm_tower_d1_rec_r8_2aadc4'

def setup_inputs(seed: int=0):
    np.random.seed(seed)
    _w = jnp.asarray

    def _rec_inputs():
        import jax
        import jax.numpy as jnp
        _tk = jax.random.key(seed)
        dense_ctx = jax.random.normal(jax.random.fold_in(_tk, 190), (1024, 16), jnp.float32)
        ids = jnp.stack([jax.random.randint(jax.random.fold_in(_tk, 200 + f), (1024,), 0, v, jnp.int32) for f, v in enumerate([125000, 125000, 1000, 125000, 1000, 1250, 12500, 1250, 1000, 12500, 125000, 1250, 12500, 1000, 1000, 1000, 12500, 125000, 1250, 1000, 125000, 1250, 1250, 1000, 1250, 125000, 1250, 12500, 12500, 12500, 125000, 1250, 1250, 1000, 12500, 125000, 125000, 1250, 1250, 12500])], axis=1)
        tbl_0 = 0.05 * jax.random.normal(jax.random.fold_in(_tk, 500 + 0), (125000, 16), jnp.float32)
        tbl_1 = 0.05 * jax.random.normal(jax.random.fold_in(_tk, 500 + 1), (125000, 16), jnp.float32)
        tbl_2 = 0.05 * jax.random.normal(jax.random.fold_in(_tk, 500 + 2), (1000, 16), jnp.float32)
        tbl_3 = 0.05 * jax.random.normal(jax.random.fold_in(_tk, 500 + 3), (125000, 16), jnp.float32)
        tbl_4 = 0.05 * jax.random.normal(jax.random.fold_in(_tk, 500 + 4), (1000, 16), jnp.float32)
        tbl_5 = 0.05 * jax.random.normal(jax.random.fold_in(_tk, 500 + 5), (1250, 16), jnp.float32)
        tbl_6 = 0.05 * jax.random.normal(jax.random.fold_in(_tk, 500 + 6), (12500, 16), jnp.float32)
        tbl_7 = 0.05 * jax.random.normal(jax.random.fold_in(_tk, 500 + 7), (1250, 16), jnp.float32)
        tbl_8 = 0.05 * jax.random.normal(jax.random.fold_in(_tk, 500 + 8), (1000, 16), jnp.float32)
        tbl_9 = 0.05 * jax.random.normal(jax.random.fold_in(_tk, 500 + 9), (12500, 16), jnp.float32)
        tbl_10 = 0.05 * jax.random.normal(jax.random.fold_in(_tk, 500 + 10), (125000, 16), jnp.float32)
        tbl_11 = 0.05 * jax.random.normal(jax.random.fold_in(_tk, 500 + 11), (1250, 16), jnp.float32)
        tbl_12 = 0.05 * jax.random.normal(jax.random.fold_in(_tk, 500 + 12), (12500, 16), jnp.float32)
        tbl_13 = 0.05 * jax.random.normal(jax.random.fold_in(_tk, 500 + 13), (1000, 16), jnp.float32)
        tbl_14 = 0.05 * jax.random.normal(jax.random.fold_in(_tk, 500 + 14), (1000, 16), jnp.float32)
        tbl_15 = 0.05 * jax.random.normal(jax.random.fold_in(_tk, 500 + 15), (1000, 16), jnp.float32)
        tbl_16 = 0.05 * jax.random.normal(jax.random.fold_in(_tk, 500 + 16), (12500, 16), jnp.float32)
        tbl_17 = 0.05 * jax.random.normal(jax.random.fold_in(_tk, 500 + 17), (125000, 16), jnp.float32)
        tbl_18 = 0.05 * jax.random.normal(jax.random.fold_in(_tk, 500 + 18), (1250, 16), jnp.float32)
        tbl_19 = 0.05 * jax.random.normal(jax.random.fold_in(_tk, 500 + 19), (1000, 16), jnp.float32)
        tbl_20 = 0.05 * jax.random.normal(jax.random.fold_in(_tk, 500 + 20), (125000, 16), jnp.float32)
        tbl_21 = 0.05 * jax.random.normal(jax.random.fold_in(_tk, 500 + 21), (1250, 16), jnp.float32)
        tbl_22 = 0.05 * jax.random.normal(jax.random.fold_in(_tk, 500 + 22), (1250, 16), jnp.float32)
        tbl_23 = 0.05 * jax.random.normal(jax.random.fold_in(_tk, 500 + 23), (1000, 16), jnp.float32)
        tbl_24 = 0.05 * jax.random.normal(jax.random.fold_in(_tk, 500 + 24), (1250, 16), jnp.float32)
        tbl_25 = 0.05 * jax.random.normal(jax.random.fold_in(_tk, 500 + 25), (125000, 16), jnp.float32)
        tbl_26 = 0.05 * jax.random.normal(jax.random.fold_in(_tk, 500 + 26), (1250, 16), jnp.float32)
        tbl_27 = 0.05 * jax.random.normal(jax.random.fold_in(_tk, 500 + 27), (12500, 16), jnp.float32)
        tbl_28 = 0.05 * jax.random.normal(jax.random.fold_in(_tk, 500 + 28), (12500, 16), jnp.float32)
        tbl_29 = 0.05 * jax.random.normal(jax.random.fold_in(_tk, 500 + 29), (12500, 16), jnp.float32)
        tbl_30 = 0.05 * jax.random.normal(jax.random.fold_in(_tk, 500 + 30), (125000, 16), jnp.float32)
        tbl_31 = 0.05 * jax.random.normal(jax.random.fold_in(_tk, 500 + 31), (1250, 16), jnp.float32)
        tbl_32 = 0.05 * jax.random.normal(jax.random.fold_in(_tk, 500 + 32), (1250, 16), jnp.float32)
        tbl_33 = 0.05 * jax.random.normal(jax.random.fold_in(_tk, 500 + 33), (1000, 16), jnp.float32)
        tbl_34 = 0.05 * jax.random.normal(jax.random.fold_in(_tk, 500 + 34), (12500, 16), jnp.float32)
        tbl_35 = 0.05 * jax.random.normal(jax.random.fold_in(_tk, 500 + 35), (125000, 16), jnp.float32)
        tbl_36 = 0.05 * jax.random.normal(jax.random.fold_in(_tk, 500 + 36), (125000, 16), jnp.float32)
        tbl_37 = 0.05 * jax.random.normal(jax.random.fold_in(_tk, 500 + 37), (1250, 16), jnp.float32)
        tbl_38 = 0.05 * jax.random.normal(jax.random.fold_in(_tk, 500 + 38), (1250, 16), jnp.float32)
        tbl_39 = 0.05 * jax.random.normal(jax.random.fold_in(_tk, 500 + 39), (12500, 16), jnp.float32)
        _rk = jax.random.fold_in(_tk, 7)
        W_top1 = 0.05 * jax.random.normal(jax.random.fold_in(_tk, 801), (400, 512), jnp.float32)
        W_top2 = 0.0441942 * jax.random.normal(jax.random.fold_in(_tk, 802), (512, 256), jnp.float32)
        W_top3 = 0.0625 * jax.random.normal(jax.random.fold_in(_tk, 803), (256, 1), jnp.float32)
        b_top1 = jnp.zeros((512,), jnp.float32)
        b_top2 = jnp.zeros((256,), jnp.float32)
        return (dense_ctx, ids, tbl_0, tbl_1, tbl_2, tbl_3, tbl_4, tbl_5, tbl_6, tbl_7, tbl_8, tbl_9, tbl_10, tbl_11, tbl_12, tbl_13, tbl_14, tbl_15, tbl_16, tbl_17, tbl_18, tbl_19, tbl_20, tbl_21, tbl_22, tbl_23, tbl_24, tbl_25, tbl_26, tbl_27, tbl_28, tbl_29, tbl_30, tbl_31, tbl_32, tbl_33, tbl_34, tbl_35, tbl_36, tbl_37, tbl_38, tbl_39, W_top1, b_top1, W_top2, b_top2, W_top3)
    dense_ctx, ids, tbl_0, tbl_1, tbl_2, tbl_3, tbl_4, tbl_5, tbl_6, tbl_7, tbl_8, tbl_9, tbl_10, tbl_11, tbl_12, tbl_13, tbl_14, tbl_15, tbl_16, tbl_17, tbl_18, tbl_19, tbl_20, tbl_21, tbl_22, tbl_23, tbl_24, tbl_25, tbl_26, tbl_27, tbl_28, tbl_29, tbl_30, tbl_31, tbl_32, tbl_33, tbl_34, tbl_35, tbl_36, tbl_37, tbl_38, tbl_39, W_top1, b_top1, W_top2, b_top2, W_top3 = _rec_inputs()

    def _L0_rec_setup():
        import jax, jax.numpy as jnp
        import numpy as np
        B, M, D = (512, 40, 16)
        DIMS = [128, 128, 128]
        key = jax.random.key(seed)
        k_x, k0, k1, k2 = jax.random.split(key, 4)
        scale = lambda fan_in: (2.0 / fan_in) ** 0.5
        x0 = jax.random.normal(k_x, (B, M, D), dtype=jnp.float32)
        kern0 = jax.random.normal(k0, (DIMS[0], M, M), dtype=jnp.float32) * scale(M * M)
        kern1 = jax.random.normal(k1, (DIMS[1], DIMS[0], M), dtype=jnp.float32) * scale(DIMS[0] * M)
        kern2 = jax.random.normal(k2, (DIMS[2], DIMS[1], M), dtype=jnp.float32) * scale(DIMS[1] * M)
        return {'x0': x0, 'k0': kern0, 'k1': kern1, 'k2': kern2}
    _L0_rec_all = _L0_rec_setup()
    _L0_rec_in = {k: v for k, v in _L0_rec_all.items() if k in ('k0', 'k1', 'k2')}
    del _L0_rec_all
    return {'dense_ctx': dense_ctx, 'ids': ids, 'tbl_0': tbl_0, 'tbl_1': tbl_1, 'tbl_2': tbl_2, 'tbl_3': tbl_3, 'tbl_4': tbl_4, 'tbl_5': tbl_5, 'tbl_6': tbl_6, 'tbl_7': tbl_7, 'tbl_8': tbl_8, 'tbl_9': tbl_9, 'tbl_10': tbl_10, 'tbl_11': tbl_11, 'tbl_12': tbl_12, 'tbl_13': tbl_13, 'tbl_14': tbl_14, 'tbl_15': tbl_15, 'tbl_16': tbl_16, 'tbl_17': tbl_17, 'tbl_18': tbl_18, 'tbl_19': tbl_19, 'tbl_20': tbl_20, 'tbl_21': tbl_21, 'tbl_22': tbl_22, 'tbl_23': tbl_23, 'tbl_24': tbl_24, 'tbl_25': tbl_25, 'tbl_26': tbl_26, 'tbl_27': tbl_27, 'tbl_28': tbl_28, 'tbl_29': tbl_29, 'tbl_30': tbl_30, 'tbl_31': tbl_31, 'tbl_32': tbl_32, 'tbl_33': tbl_33, 'tbl_34': tbl_34, 'tbl_35': tbl_35, 'tbl_36': tbl_36, 'tbl_37': tbl_37, 'tbl_38': tbl_38, 'tbl_39': tbl_39, 'W_top1': W_top1, 'b_top1': b_top1, 'W_top2': W_top2, 'b_top2': b_top2, 'W_top3': W_top3, 'L0_rec_k0': _L0_rec_in['k0'], 'L0_rec_k1': _L0_rec_in['k1'], 'L0_rec_k2': _L0_rec_in['k2']}

def reference(dense_ctx, ids, tbl_0, tbl_1, tbl_2, tbl_3, tbl_4, tbl_5, tbl_6, tbl_7, tbl_8, tbl_9, tbl_10, tbl_11, tbl_12, tbl_13, tbl_14, tbl_15, tbl_16, tbl_17, tbl_18, tbl_19, tbl_20, tbl_21, tbl_22, tbl_23, tbl_24, tbl_25, tbl_26, tbl_27, tbl_28, tbl_29, tbl_30, tbl_31, tbl_32, tbl_33, tbl_34, tbl_35, tbl_36, tbl_37, tbl_38, tbl_39, W_top1, b_top1, W_top2, b_top2, W_top3, L0_rec_k0, L0_rec_k1, L0_rec_k2):
    import jax
    import jax.numpy as jnp

    def _L0_rec_ref(x0, k0, k1, k2):
        import jax, jax.numpy as jnp
        import numpy as np
        B, M, D = (512, 40, 16)
        DIMS = [128, 128, 128]
        x = x0
        outputs = []
        for k in (k0, k1, k2):
            x = jnp.einsum('bhd,bmd,ohm->bod', x, x0, k)
            outputs.append(jnp.sum(x, axis=-1))
        return jnp.concatenate(outputs, axis=1)
    e = jnp.stack([tbl_0[ids[:, 0]], tbl_1[ids[:, 1]], tbl_2[ids[:, 2]], tbl_3[ids[:, 3]], tbl_4[ids[:, 4]], tbl_5[ids[:, 5]], tbl_6[ids[:, 6]], tbl_7[ids[:, 7]], tbl_8[ids[:, 8]], tbl_9[ids[:, 9]], tbl_10[ids[:, 10]], tbl_11[ids[:, 11]], tbl_12[ids[:, 12]], tbl_13[ids[:, 13]], tbl_14[ids[:, 14]], tbl_15[ids[:, 15]], tbl_16[ids[:, 16]], tbl_17[ids[:, 17]], tbl_18[ids[:, 18]], tbl_19[ids[:, 19]], tbl_20[ids[:, 20]], tbl_21[ids[:, 21]], tbl_22[ids[:, 22]], tbl_23[ids[:, 23]], tbl_24[ids[:, 24]], tbl_25[ids[:, 25]], tbl_26[ids[:, 26]], tbl_27[ids[:, 27]], tbl_28[ids[:, 28]], tbl_29[ids[:, 29]], tbl_30[ids[:, 30]], tbl_31[ids[:, 31]], tbl_32[ids[:, 32]], tbl_33[ids[:, 33]], tbl_34[ids[:, 34]], tbl_35[ids[:, 35]], tbl_36[ids[:, 36]], tbl_37[ids[:, 37]], tbl_38[ids[:, 38]], tbl_39[ids[:, 39]]], axis=1)
    z = _L0_rec_ref(e, L0_rec_k0, L0_rec_k1, L0_rec_k2)
    z = z.reshape(z.shape[0], -1)
    h = jnp.concatenate([z, dense_ctx], axis=1)
    h = jnp.maximum(h @ W_top1 + b_top1, 0.0)
    h = jnp.maximum(h @ W_top2 + b_top2, 0.0)
    y = h @ W_top3
    return y

_drawn_inputs = setup_inputs


def setup_inputs(seed=0):
    import zlib

    import numpy as np

    out = dict(_drawn_inputs(seed))
    spreads = {'b_top1': (0.0, 0.463), 'b_top2': (0.0, 0.1)}
    factors = {'tbl_0': 7.225,
     'tbl_1': 6.693,
     'tbl_2': 6.488,
     'tbl_3': 6.863,
     'tbl_4': 6.977,
     'tbl_5': 7.146,
     'tbl_6': 6.997,
     'tbl_7': 7.66,
     'tbl_8': 6.434,
     'tbl_9': 6.551,
     'tbl_10': 6.783,
     'tbl_11': 6.714,
     'tbl_12': 6.495,
     'tbl_13': 6.634,
     'tbl_14': 7.366,
     'tbl_15': 6.895,
     'tbl_16': 7.123,
     'tbl_17': 6.063,
     'tbl_18': 6.917,
     'tbl_19': 6.436,
     'tbl_20': 6.878,
     'tbl_21': 7.544,
     'tbl_22': 6.765,
     'tbl_23': 6.27,
     'tbl_24': 7.213,
     'tbl_25': 6.663,
     'tbl_26': 6.995,
     'tbl_27': 6.731,
     'tbl_28': 6.422,
     'tbl_29': 6.811,
     'tbl_30': 7.0,
     'tbl_31': 6.749,
     'tbl_32': 7.328,
     'tbl_33': 6.08,
     'tbl_34': 6.711,
     'tbl_35': 6.146,
     'tbl_36': 6.643,
     'tbl_37': 6.435,
     'tbl_38': 6.928,
     'tbl_39': 6.595,
     'L0_rec_k1': 8.0,
     'L0_rec_k2': 8.0}
    for name, (base, spread) in spreads.items():
        noise = np.random.default_rng([zlib.crc32(name.encode()), seed]).standard_normal(out[name].shape)
        drawn = base * np.exp(spread * noise) if base else spread * noise
        out[name] = jnp.asarray(drawn.astype(out[name].dtype))
    for name, factor in factors.items():
        out[name] = (out[name] * factor).astype(out[name].dtype)
    return out
```

```python
from contextlib import ExitStack

import concourse.bass as bass
from concourse import mybir

B, M, D, O = 1024, 40, 16, 128
F_DENSE, H1, H2 = 16, 512, 256
GB = 32
GN = GB * D
NG = B // GB
TB = 128 // D
NT = GB // TB
QB = 256
QG = QB // GB
NQ = B // QB
LB = 128
LG = LB // GB
NL = B // LB
MC = 4
NC = M // MC
ROT = M // 2 + 1
RC = 3
NP = ROT // RC
PR = RC * M
LO = 64
XR = LO + M
M1 = M + 1

VEC = [c for c in range(NC) if c % 2 == 0]
SCA = [c for c in range(NC) if c % 2 == 1]
NV, NS = len(VEC), len(SCA)
FREE = 2
YB = 4


def cin_tower(nc, ids, tables, dense_t, k0_pairs, k0_swapped, k1_t, k2_t, w1_z, w1_dense, b1, w2, b2, w3,
              select, block_mask, identity, out):
    f32, f32r, i32 = mybir.dt.float32, mybir.dt.float32r, mybir.dt.int32
    ALU, ACT, AX = mybir.AluOpType, mybir.ActivationFunctionType, mybir.AxisListType
    ds = bass.ds

    x0_rows = nc.dram_tensor("x0_rows", (M, B, D), f32, kind="Internal").ap()

    with ExitStack() as ctx:
        def sb(name, shape, dt=f32):
            return ctx.enter_context(nc.sbuf_tensor(name, shape, dt))

        def bank(name):
            return ctx.enter_context(nc.psum_tensor(name, [128, 512], f32))

        def sem(name):
            return ctx.enter_context(nc.semaphore(name))

        k1_hi, k1_lo = sb("k1_hi", [O, M * O], f32r), sb("k1_lo", [O, M * O], f32r)
        k2_sb = sb("k2_sb", [O, M, O])
        w0 = sb("w0", [PR, NP, O])
        w1_sb, w1d_sb = sb("w1_sb", [O, 3, H1]), sb("w1d_sb", [F_DENSE, H1])
        w2_sb, w3_sb = sb("w2_sb", [128, H1 // 128, H2]), sb("w3_sb", [128, H2 // 128])
        b1_sb, b2_sb = sb("b1_sb", [128, H1 // 128]), sb("b2_sb", [128, H2 // 128])
        dense_sb = sb("dense_sb", [F_DENSE, B])
        sel = sb("sel", [XR, (1 + NP) * PR], f32r)
        mask = sb("mask", [128, TB])
        ident = sb("ident", [M, M])
        idx = sb("idx", [LB, M], i32)
        rows = sb("rows", [LB, M * D])
        x = sb("x", [XR, GN])
        xs = sb("xs", [XR, GN], f32r)
        xa = sb("xa", [PR, GN])
        pairs = sb("pairs", [PR, NP, GN])
        x1_hi, x1_lo = sb("x1_hi", [O, GN], f32r), sb("x1_lo", [O, GN], f32r)
        x0t = sb("x0t", [128, NT, M1])
        acc = sb("acc", [128, 2, MC, O])
        terms = sb("terms", [128, 2, NS, MC * O])
        total = sb("total", [128, MC, O])
        x2 = sb("x2", [128, 2, O])
        blocks = sb("blocks", [128, 2, TB, M1])
        gram = sb("gram", [O, M1, QB])
        z0 = sb("z0", [O, B])
        z2 = sb("z2", [O, QB])
        h1, h2 = sb("h1", [128, H1 // 128, QB]), sb("h2", [128, H2 // 128, QB])
        y_sb = sb("y_sb", [1, B])
        raw = gram[:, :, :].rearrange("h m b -> h (m b)")
        k1_raw = raw[:, 0:M * O]
        w0_raw = raw[0:PR, M * O:M * O + NP * O]
        sel_raw = raw[0:XR, M * O + NP * O:M * O + NP * O + (1 + NP) * PR]

        y_ps = [bank(f"y_ps{i}") for i in range(YB)]
        rot_ps = [bank(f"rot_ps{i}") for i in range(2)]
        x1_ps = bank("x1_ps")
        gram_ps = bank("gram_ps")

        ids_loaded, gathered, rows_stored = sem("ids_loaded"), sem("gathered"), sem("rows_stored")
        x_loaded, out_stored = sem("x_loaded"), sem("out_stored")
        k1_loaded, w0_loaded, sel_loaded, small_loaded = (sem("k1_loaded"), sem("w0_loaded"), sem("sel_loaded"),
                                                          sem("small_loaded"))
        late_loaded = sem("late_loaded")
        x_zeroed, ones_set = sem("x_zeroed"), sem("ones_set")
        sel_ready, k1_hi_ready, k1_lo_ready, w0_ready = (sem("sel_ready"), sem("k1_hi_ready"), sem("k1_lo_ready"),
                                                         sem("w0_ready"))
        xs_rounded, xs_ready = sem("xs_rounded"), sem("xs_ready")
        xa_made, xa_ready = sem("xa_made"), sem("xa_ready")
        rot_made, pairs_ready = sem("rot_made"), sem("pairs_ready")
        x1_made, x1_hi_ready, x1_lo_ready, z0_ready = (sem("x1_made"), sem("x1_hi_ready"), sem("x1_lo_ready"),
                                                       sem("z0_ready"))
        x0t_made, x0t_ready = sem("x0t_made"), sem("x0t_ready")
        y_made = sem("y_made")
        y_used_vec = sem("y_used_vec")
        y_used_sca = sem("y_used_sca")
        terms_added = sem("terms_added")
        terms_used = sem("terms_used")
        x2_ready, blocks_ready = sem("x2_ready"), sem("blocks_ready")
        gram_made, gram_kept = sem("gram_made"), sem("gram_kept")
        z2_made, z2_ready = sem("z2_made"), sem("z2_ready")
        h1_made, h1_ready = sem("h1_made"), sem("h1_ready")
        h2_made, h2_ready = sem("h2_made"), sem("h2_ready")
        y_out_made, y_out_ready = sem("y_out_made"), sem("y_out_ready")

        def after_first(g):
            return not isinstance(g, int) or g > 0

        block = ctx.enter_context(nc.Block())

        @block.sync
        def _(sp):
            def load_ids(t):
                sp.dma_start(idx[:, :], ids[ds(t * LB, LB), :]).then_inc(ids_loaded, 16)

            def lookup_block(t, more):
                sp.wait_ge(gathered, (t + 1) * (M * 16))
                sp.dma_start(x0_rows[:, ds(t * LB, LB), :].rearrange("m b d -> b m d"),
                             rows[:, :].rearrange("b (m d) -> b m d", m=M)).then_inc(rows_stored, 16)
                if more:
                    load_ids(t + 1)
                for i in range(LG):
                    g = t * LG + i
                    sp.wait_ge(x0t_made, g + 1)
                    if i == 0:
                        sp.wait_ge(rows_stored, t * 16 + 16)
                    for r in (0, LO):
                        sp.dma_start(x[r:r + M, :], x0_rows[:, ds(g * GB, GB), :].rearrange("m b d -> m (b d)")
                                     ).then_inc(x_loaded, 16)

            load_ids(0)
            sp.dma_start(sel_raw, select).then_inc(sel_loaded, 16)
            sp.dma_start(w0[:, :, :], k0_pairs).then_inc(w0_loaded, 16)
            sp.dma_start(w0_raw, k0_swapped.rearrange("p c o -> p (c o)")).then_inc(w0_loaded, 16)
            sp.dma_start(mask[:, :], block_mask).then_inc(small_loaded, 16)
            sp.dma_start(ident[:, :], identity).then_inc(small_loaded, 16)
            sp.dma_start(k1_raw, k1_t).then_inc(k1_loaded, 16)
            sp.dma_start(k2_sb[:, :, :], k2_t).then_inc(late_loaded, 16)
            sp.dma_start(w1_sb[:, :, :], w1_z).then_inc(late_loaded, 16)
            sp.dma_start(w1d_sb[:, :], w1_dense).then_inc(late_loaded, 16)
            sp.dma_start(w2_sb[:, :, :], w2).then_inc(late_loaded, 16)
            sp.dma_start(w3_sb[:, :], w3).then_inc(late_loaded, 16)
            sp.dma_start(b1_sb[:, :], b1).then_inc(late_loaded, 16)
            sp.dma_start(b2_sb[:, :], b2).then_inc(late_loaded, 16)
            sp.dma_start(dense_sb[:, :], dense_t).then_inc(late_loaded, 16)
            sp.wait_ge(x_zeroed, 1)
            with sp.Fori(0, NL - 1) as t:
                lookup_block(t, True)
            lookup_block(NL - 1, False)
            sp.wait_ge(y_out_ready, NQ)
            sp.dma_start(out, y_sb[:, :]).then_inc(out_stored, 16)
            sp.wait_ge(out_stored, 16)

        @block.gpsimd
        def _(pool):
            def gather(t, m):
                nc.gpsimd.indirect_dma_start(
                    rows[:, m * D:(m + 1) * D], None, tables[m],
                    bass.IndirectOffsetOnAxis(ap=idx[:, m:m + 1], axis=0)).then_inc(gathered, 16)

            def wait_gather(t):
                pool.wait_ge(ids_loaded, (t + 1) * 16)
                pool.wait_ge(rows_stored, t * 16)

            def tile(t, i, tables_now):
                g, j, p = t * LG + i // NT, i % NT, i % 2
                k = t * (LG * NT) + i
                if j == 0:
                    pool.wait_ge(x0t_ready, g + 1)
                if 0 in tables_now:
                    wait_gather(t + 1)
                pool.wait_ge(gram_kept, k + 1)
                nc.gpsimd.tensor_tensor(
                    blocks[:, p], x0t[:, j, :].unsqueeze(1).to_broadcast([128, TB, M1]),
                    mask[:, :].unsqueeze(2).to_broadcast([128, TB, M1]), ALU.mult).then_inc(blocks_ready, 1)
                for s in range(1, NS):
                    for m in tables_now[s - 1::NS - 1]:
                        gather(t + 1, m)
                    pool.wait_ge(y_used_sca, k * NS + FREE + s + 1)
                    if s > 1:
                        pool.wait_ge(terms_added, k * (NS - 1) + s - 1)
                    nc.gpsimd.tensor_tensor(terms[:, p, 0], terms[:, p, 0], terms[:, p, s],
                                            ALU.add).then_inc(terms_added, 1)

            def lookup_block(t, more):
                tiles = LG * NT
                spread = 3 * tiles // 4
                for i in range(tiles):
                    now = range(i * M // spread, (i + 1) * M // spread) if more and i < spread else ()
                    tile(t, i, list(now))

            nc.gpsimd.memset(x0t[:, :, M:M1], 1.0).then_inc(ones_set, 1)
            pool.wait_ge(ids_loaded, 16)
            for m in range(M):
                gather(0, m)
            pool.wait_ge(small_loaded, 32)
            pool.wait_ge(ones_set, 1)
            with pool.Fori(0, NL - 1) as t:
                lookup_block(t, True)
            lookup_block(NL - 1, False)

        @block.tensor
        def _(pe):
            def repeat_x0(g):
                pe.wait_ge(xs_ready, g + 1)
                if after_first(g):
                    pe.wait_ge(z0_ready, g)
                nc.tensor.matmul(x1_ps[0:PR, :], sel[:, 0:PR], xs[:, :], start=True, stop=True).then_inc(xa_made, 1)

            def rotate_x0(g, c):
                if c == 1 and after_first(g):
                    pe.wait_ge(x0t_ready, g)
                if c >= 2:
                    pe.wait_ge(pairs_ready, g * NP + c - 1)
                nc.tensor.matmul(rot_ps[c % 2][0:PR, :], sel[:, (1 + c) * PR:(2 + c) * PR], xs[:, :],
                                 start=True, stop=True).then_inc(rot_made, 1)

            def first_layer(g):
                for c in range(NP):
                    pe.wait_ge(pairs_ready, g * NP + c + 1)
                    ins = nc.tensor.matmul(x1_ps[:, :], w0[:, c, :], pairs[:, c, :], start=c == 0, stop=c == NP - 1)
                ins.then_inc(x1_made, 1)

            def transpose_x0(g):
                for j in range(NT):
                    ins = nc.tensor.transpose(rot_ps[1][:, j * M:(j + 1) * M], x[0:M, j * 128:(j + 1) * 128],
                                              ident[:, :])
                ins.then_inc(x0t_made, 1)

            def second_layer(g, j, c):
                s = j * NC + c
                if s == 0:
                    pe.wait_ge(x1_hi_ready, g + 1)
                if c in VEC:
                    pe.wait_ge(y_used_vec, g * (NT * NV) + j * NV + VEC.index(c) + 1)
                else:
                    pe.wait_ge(y_used_sca, g * (NT * NS) + j * NS + SCA.index(c) + 1)
                ps, n, k = y_ps[s % YB], slice(j * 128, (j + 1) * 128), slice(c * MC * O, (c + 1) * MC * O)
                nc.tensor.matmul(ps[:, :], x1_hi[:, n], k1_hi[:, k], start=True, stop=False)
                nc.tensor.matmul(ps[:, :], x1_hi[:, n], k1_lo[:, k], start=False, stop=False)
                if s == 0:
                    pe.wait_ge(x1_lo_ready, g + 1)
                nc.tensor.matmul(ps[:, :], x1_lo[:, n], k1_hi[:, k], start=False, stop=True).then_inc(y_made, 1)

            def gram_of_tile(g, j):
                k = g * NT + j
                pe.wait_ge(x2_ready, k + 2)
                pe.wait_ge(blocks_ready, k + 1)
                pe.wait_ge(gram_kept, k + FREE)
                nc.tensor.matmul(gram_ps[:, 0:TB * M1], x2[:, j % 2],
                                 blocks[:, j % 2].rearrange("n b m -> n (b m)"), start=True, stop=True
                                 ).then_inc(gram_made, 1)

            def group(g, more):
                for j in range(NT):
                    for c in range(NC):
                        s = j * NC + c
                        if more and s == 9:
                            repeat_x0(g + 1)
                        if more and s >= 12 and s % 4 == 0 and (s - 12) // 4 < NP:
                            rotate_x0(g + 1, (s - 12) // 4)
                        second_layer(g, j, c)
                        if c == 8 and j > 0:
                            gram_of_tile(g, j - 1)
                if more:
                    first_layer(g + 1)
                    transpose_x0(g + 1)
                gram_of_tile(g, NT - 1)

            def third_layer_and_mlp(q):
                pe.wait_ge(gram_kept, (q + 1) * (QG * NT) + FREE)
                zp = gram_ps[:, 0:QB]
                for m in range(M):
                    ins = nc.tensor.matmul(zp, k2_sb[:, m, :], gram[:, m, :], start=m == 0, stop=m == M - 1)
                ins.then_inc(z2_made, 1)
                cols = ds(q * QB, QB)
                for o in range(H1 // 128):
                    f = slice(o * 128, (o + 1) * 128)
                    hp = y_ps[o][:, 0:QB]
                    nc.tensor.matmul(hp, w1_sb[:, 0, f], z0[:, cols], start=True, stop=False)
                    nc.tensor.matmul(hp, w1_sb[:, 1, f], gram[:, M, :], start=False, stop=False)
                    nc.tensor.matmul(hp, w1d_sb[:, f], dense_sb[:, cols], start=False, stop=False)
                pe.wait_ge(z2_ready, q + 1)
                for o in range(H1 // 128):
                    nc.tensor.matmul(y_ps[o][:, 0:QB], w1_sb[:, 2, o * 128:(o + 1) * 128], z2[:, :],
                                     start=False, stop=True).then_inc(h1_made, 1)
                for i in range(H1 // 128):
                    pe.wait_ge(h1_ready, q * (H1 // 128) + i + 1)
                    for o in range(H2 // 128):
                        ins = nc.tensor.matmul(rot_ps[o][:, 0:QB], w2_sb[:, i, o * 128:(o + 1) * 128], h1[:, i, :],
                                               start=i == 0, stop=i == H1 // 128 - 1)
                        if i == H1 // 128 - 1:
                            ins.then_inc(h2_made, 1)
                for i in range(H2 // 128):
                    pe.wait_ge(h2_ready, q * (H2 // 128) + i + 1)
                    ins = nc.tensor.matmul(gram_ps[0:1, 0:QB], w3_sb[:, i:i + 1], h2[:, i, :],
                                           start=i == 0, stop=i == H2 // 128 - 1)
                ins.then_inc(y_out_made, 1)
                pe.wait_ge(y_out_ready, q + 1)

            pe.sem_inc(x0t_made, 1)
            pe.wait_ge(sel_ready, 1)
            repeat_x0(0)
            for c in range(NP):
                rotate_x0(0, c)
            pe.wait_ge(w0_ready, 1)
            first_layer(0)
            pe.wait_ge(small_loaded, 32)
            transpose_x0(0)
            pe.wait_ge(k1_hi_ready, 1)
            pe.wait_ge(k1_lo_ready, 1)
            with pe.Fori(0, NQ - 1) as q:
                with pe.Fori(0, QG) as i:
                    group(q * QG + i, True)
                pe.wait_ge(late_loaded, 8 * 16)
                third_layer_and_mlp(q)
            with pe.Fori(0, QG - 1) as i:
                group(i + (NQ - 1) * QG, True)
            group(NG - 1, False)
            third_layer_and_mlp(NQ - 1)

        @block.scalar
        def _(act):
            def round_x0(g):
                act.wait_ge(x_loaded, (g + 1) * 32)
                nc.scalar.activation(xs[:, :], x[:, :], ACT.Copy).then_inc(xs_rounded, 1)

            def keep_repeated(g):
                act.wait_ge(xa_made, g + 1)
                if after_first(g):
                    act.wait_ge(pairs_ready, g * NP)
                nc.scalar.activation(xa[:, :], x1_ps[0:PR, :], ACT.Copy).then_inc(xa_ready, 1)

            def round_x1(g):
                act.wait_ge(x1_made, g + 1)
                nc.scalar.activation(x1_hi[:, :], x1_ps[:, :], ACT.Copy).then_inc(x1_hi_ready, 1)

            def keep_x0t(g):
                act.wait_ge(x0t_made, g + 2)
                if after_first(g):
                    act.wait_ge(y_used_vec, g * (NT * NV) + FREE)
                    act.wait_ge(y_used_sca, g * (NT * NS) + FREE)
                    act.wait_ge(blocks_ready, g * NT)
                nc.scalar.activation(x0t[:, :, 0:M], rot_ps[1][:, 0:NT * M].rearrange("n (j m) -> n j m", j=NT),
                                     ACT.Copy).then_inc(x0t_ready, 1)

            def weight_chunk(g, j, i):
                c = SCA[i]
                if i == 0:
                    act.wait_ge(terms_used, g * NT + j + 1)
                act.wait_ge(y_made, g * (NT * NC) + j * NC + c + 1)
                for r in range(MC):
                    m = c * MC + r
                    ins = nc.scalar.activation(terms[:, j % 2, i, r * O:(r + 1) * O],
                                               y_ps[(j * NC + c) % YB][:, r * O:(r + 1) * O], ACT.Copy,
                                               scale=x0t[:, j, m:m + 1])
                ins.then_inc(y_used_sca, 1)

            def keep_gram(g, i, j):
                k = g * NT + j
                act.wait_ge(gram_made, k + 1)
                nc.scalar.activation(gram[:, :, ds(i * GB + j * TB, TB)],
                                     gram_ps[:, 0:TB * M1].rearrange("h (b m) -> h m b", b=TB),
                                     ACT.Copy).then_inc(gram_kept, 1)

            def group(g, i, more):
                act.wait_ge(x0t_ready, g + 1)
                for j in range(NT):
                    for n in range(NS):
                        weight_chunk(g, j, n)
                        s = j * NC + SCA[n]
                        if more and s == 5:
                            round_x0(g + 1)
                        if more and s == 11:
                            keep_repeated(g + 1)
                    if j > 0:
                        keep_gram(g, i, j - 1)
                if more:
                    round_x1(g + 1)
                    keep_x0t(g + 1)
                keep_gram(g, i, NT - 1)

            def mlp(q):
                act.wait_ge(z2_made, q + 1)
                nc.scalar.activation(z2[:, :], gram_ps[:, 0:QB], ACT.Copy).then_inc(z2_ready, 1)
                for o in range(H1 // 128):
                    act.wait_ge(h1_made, q * (H1 // 128) + o + 1)
                    nc.scalar.activation(h1[:, o, :], y_ps[o][:, 0:QB], ACT.Relu,
                                         bias=b1_sb[:, o:o + 1]).then_inc(h1_ready, 1)
                for o in range(H2 // 128):
                    act.wait_ge(h2_made, q * (H2 // 128) + o + 1)
                    nc.scalar.activation(h2[:, o, :], rot_ps[o][:, 0:QB], ACT.Relu,
                                         bias=b2_sb[:, o:o + 1]).then_inc(h2_ready, 1)
                act.wait_ge(y_out_made, q + 1)
                nc.scalar.activation(y_sb[:, ds(q * QB, QB)], gram_ps[0:1, 0:QB], ACT.Copy).then_inc(y_out_ready, 1)

            act.sem_inc(y_used_sca, FREE)
            act.sem_inc(gram_kept, FREE)
            act.wait_ge(sel_loaded, 16)
            nc.scalar.activation(sel[:, :], sel_raw, ACT.Copy).then_inc(sel_ready, 1)
            act.wait_ge(k1_loaded, 16)
            nc.scalar.activation(k1_hi[:, :], k1_raw, ACT.Copy).then_inc(k1_hi_ready, 1)
            round_x0(0)
            keep_repeated(0)
            round_x1(0)
            act.wait_ge(ones_set, 1)
            keep_x0t(0)
            with act.Fori(0, NQ - 1) as q:
                with act.Fori(0, QG) as i:
                    group(q * QG + i, i, True)
                act.wait_ge(late_loaded, 8 * 16)
                mlp(q)
            with act.Fori(0, QG - 1) as i:
                group(i + (NQ - 1) * QG, i, True)
            group(NG - 1, QG - 1, False)
            mlp(NQ - 1)

        @block.vector
        def _(dve):
            def low_x0(g):
                dve.wait_ge(xs_rounded, g + 1)
                nc.vector.tensor_tensor(xs[LO:XR, :], x[LO:XR, :], xs[LO:XR, :].bitcast(f32),
                                        ALU.subtract).then_inc(xs_ready, 1)

            def pair_products(g, c):
                if c == 0:
                    dve.wait_ge(xa_ready, g + 1)
                    if after_first(g):
                        dve.wait_ge(x1_made, g)
                dve.wait_ge(rot_made, g * NP + c + 1)
                nc.vector.tensor_tensor(pairs[:, c, :], rot_ps[c % 2][0:PR, :], xa[:, :],
                                        ALU.mult).then_inc(pairs_ready, 1)

            def low_x1(g):
                dve.wait_ge(x1_hi_ready, g + 1)
                nc.vector.tensor_tensor(x1_lo[:, :], x1_ps[:, :], x1_hi[:, :].bitcast(f32),
                                        ALU.subtract).then_inc(x1_lo_ready, 1)
                nc.vector.tensor_reduce(z0[:, ds(g * GB, GB)], x1_ps[:, :].rearrange("o (b d) -> o b d", d=D),
                                        AX.X, ALU.add).then_inc(z0_ready, 1)

            def weight_chunk(g, j, i):
                c, p = VEC[i], j % 2
                done = g * (NT * NV) + j * NV + i + FREE
                dve.wait_ge(y_made, g * (NT * NC) + j * NC + c + 1)
                y = y_ps[(j * NC + c) % YB]
                if i == 0:
                    dve.wait_ge(terms_used, g * NT + j + 1)
                    nc.vector.tensor_tensor(acc[:, p], y[:, :].rearrange("n (m o) -> n m o", m=MC),
                                            x0t[:, j, c * MC:(c + 1) * MC].unsqueeze(2).to_broadcast([128, MC, O]),
                                            ALU.mult).then_inc(y_used_vec, 1)
                    return
                dve.wait_ge(y_used_vec, done)
                for r in range(MC):
                    m = c * MC + r
                    ins = nc.vector.scalar_tensor_tensor(acc[:, p, r], y[:, r * O:(r + 1) * O], x0t[:, j, m:m + 1],
                                                         acc[:, p, r], ALU.mult, ALU.add)
                ins.then_inc(y_used_vec, 1)

            def add_terms(g, j):
                k, p = g * NT + j, j % 2
                dve.wait_ge(y_used_vec, (k + 1) * NV + FREE)
                dve.wait_ge(terms_added, (k + 1) * (NS - 1))
                dve.wait_ge(x2_ready, k + 1)
                nc.vector.tensor_tensor(total[:, :, :].rearrange("n r o -> n (r o)"),
                                        acc[:, p].rearrange("n r o -> n (r o)"), terms[:, p, 0],
                                        ALU.add).then_inc(terms_used, 1)

            def sum_total(g, j):
                k, p = g * NT + j, j % 2
                dve.wait_ge(terms_used, k + 1 + FREE)
                dve.wait_ge(gram_kept, k + 1)
                nc.vector.tensor_reduce(x2[:, p, :], total[:, :, :].rearrange("n r o -> n o r"), AX.X,
                                        ALU.add).then_inc(x2_ready, 1)

            def group(g, more):
                dve.wait_ge(x0t_ready, g + 1)
                for j in range(NT):
                    for n in range(NV):
                        weight_chunk(g, j, n)
                        s = j * NC + VEC[n]
                        if more and s == 4:
                            low_x0(g + 1)
                        if more and s >= 14 and (s - 14) % 4 == 0 and (s - 14) // 4 < NP:
                            pair_products(g + 1, (s - 14) // 4)
                        if j > 0 and n == 1:
                            add_terms(g, j - 1)
                        if j > 0 and n == 2:
                            sum_total(g, j - 1)
                add_terms(g, NT - 1)
                sum_total(g, NT - 1)
                if more:
                    low_x1(g + 1)

            dve.sem_inc(y_used_vec, FREE)
            dve.sem_inc(terms_used, FREE)
            dve.sem_inc(x2_ready, 1)
            nc.vector.memset(x[:, :], 0.0).then_inc(x_zeroed, 1)
            dve.wait_ge(w0_loaded, 32)
            nc.vector.tensor_tensor(w0[:, :, :].rearrange("p c o -> p (c o)"),
                                    w0[:, :, :].rearrange("p c o -> p (c o)"), w0_raw, ALU.add).then_inc(w0_ready, 1)
            dve.wait_ge(k1_hi_ready, 1)
            nc.vector.tensor_tensor(k1_lo[:, :], k1_raw, k1_hi[:, :].bitcast(f32), ALU.subtract
                                    ).then_inc(k1_lo_ready, 1)
            low_x0(0)
            for c in range(NP):
                pair_products(0, c)
            low_x1(0)
            with dve.Fori(0, NG - 1) as g:
                group(g, True)
            group(NG - 1, False)


def kernel(**inputs):
    import numpy as np
    import concourse.bacc as bacc
    from concourse.bass_utils import run_bass_kernel_spmd

    def host(name):
        return np.ascontiguousarray(inputs[name])

    k0 = host("L0_rec_k0")
    h = np.arange(M)
    k0_pairs = np.zeros((PR, NP, O), k0.dtype)
    k0_swapped = np.zeros((PR, NP, O), k0.dtype)
    select = np.zeros((XR, 1 + NP, PR), np.float32)
    for a in range(RC):
        at = slice(a * M, (a + 1) * M)
        for first in (0, LO):
            select[first + h, 0, a * M + h] = 1
        for c in range(NP):
            r = RC * c + a
            m = (h + r) % M
            k0_pairs[at, c] = k0[:, h, m].T
            if 0 < r < M // 2:
                k0_swapped[at, c] = k0[:, m, h].T
            for first in (0, LO):
                select[first + m, 1 + c, a * M + h] = 1
    block_mask = np.repeat(np.eye(TB, dtype=np.float32), D, axis=0)

    w1 = host("W_top1")
    arrays = {
        "ids": host("ids"),
        "dense_t": host("dense_ctx").T,
        "k0_pairs": k0_pairs,
        "k0_swapped": k0_swapped,
        "k1_t": host("L0_rec_k1").transpose(1, 2, 0).reshape(O, M * O),
        "k2_t": host("L0_rec_k2").transpose(1, 2, 0),
        "w1_z": w1[:3 * O].reshape(3, O, H1).transpose(1, 0, 2),
        "w1_dense": w1[3 * O:],
        "b1": host("b_top1").reshape(H1 // 128, 128).T,
        "w2": host("W_top2").reshape(H1 // 128, 128, H2).transpose(1, 0, 2),
        "b2": host("b_top2").reshape(H2 // 128, 128).T,
        "w3": host("W_top3").reshape(H2 // 128, 128).T,
        "select": select.reshape(XR, (1 + NP) * PR),
        "block_mask": block_mask,
        "identity": np.eye(M, dtype=np.float32),
    }
    for m in range(M):
        arrays[f"tbl_{m}"] = host(f"tbl_{m}")
    arrays = {f"in_{k}": np.ascontiguousarray(v) for k, v in arrays.items()}

    nc = bacc.Bacc("TRN2", target_bir_lowering=False, num_devices=1)
    aps = {k[3:]: nc.dram_tensor(k, v.shape, mybir.dt.from_np(v.dtype), kind="ExternalInput").ap()
           for k, v in arrays.items()}
    tables = [aps.pop(f"tbl_{m}") for m in range(M)]
    out = nc.dram_tensor("out", (1, B), mybir.dt.float32, kind="ExternalOutput").ap()
    cin_tower(nc, tables=tables, out=out, **aps)
    result = run_bass_kernel_spmd(nc, [arrays], core_ids=[0])
    return result.results[0]["out"].reshape(B, 1)
```

```python
from contextlib import ExitStack

import concourse.bass as bass
from concourse import mybir

B, M, D, O = 1024, 40, 16, 128
F_DENSE, H1, H2 = 16, 512, 256
GB = 32
GN = GB * D
NG = B // GB
TB = 128 // D
NT = GB // TB
QB = 256
QG = QB // GB
NQ = B // QB
LB = 128
LG = LB // GB
LT = LG * NT
NL = B // LB
MC = 4
NC = M // MC
ROT = M // 2 + 1
RC = 3
NP = ROT // RC
PR = RC * M
WRAP = ROT - 1
M1 = M + 1

VEC = [0, 3, 5, 8]
SCA = [1, 2, 4, 6, 7, 9]
NV, NS = len(VEC), len(SCA)
NA = [4, 4, 4, 3]
LAST = sum(NS - 1 - n for n in NA)
YB = 5
PAIR_SLOTS = [(0, 2), (0, 3), (1, 0), (1, 2), (2, 0), (2, 2), (3, 0)]
GRAM_AT = 4
LOOKUPS_3 = [5, 4, 4, 1, 5, 4, 4, 1, 5, 4, 3, 0]
LOOKUPS_4 = [0, 3, 3, 1, 4, 3, 3, 1, 4, 3, 3, 1, 4, 4, 3, 0]
FREE = 4


def taken(chunks, s):
    return s // NC * len(chunks) + sum(c < s % NC for c in chunks)


def cin_tower(nc, ids, tables, dense_t, k0_pairs, k0_swapped, k1_t, k2_t, w1_z, w1_dense, b1, w2, b2, w3,
              block_mask, identity, out):
    f32, f32r, i32 = mybir.dt.float32, mybir.dt.float32r, mybir.dt.int32
    ALU, ACT, AX = mybir.AluOpType, mybir.ActivationFunctionType, mybir.AxisListType
    ds = bass.ds

    x0_rows = nc.dram_tensor("x0_rows", (M + WRAP, B, D), f32, kind="Internal").ap()

    with ExitStack() as ctx:
        def sb(name, shape, dt=f32):
            return ctx.enter_context(nc.sbuf_tensor(name, shape, dt))

        def bank(name):
            return ctx.enter_context(nc.psum_tensor(name, [128, 512], f32))

        def sem(name):
            return ctx.enter_context(nc.semaphore(name))

        k1_hi, k1_lo = sb("k1_hi", [O, M * O], f32r), sb("k1_lo", [O, M * O], f32r)
        k2_sb = sb("k2_sb", [O, M, O])
        w0 = sb("w0", [PR, NP, O])
        w1_sb, w1d_sb = sb("w1_sb", [O, 3, H1]), sb("w1d_sb", [F_DENSE, H1])
        w2_sb, w3_sb = sb("w2_sb", [128, H1 // 128, H2]), sb("w3_sb", [128, H2 // 128])
        b1_sb, b2_sb = sb("b1_sb", [128, H1 // 128]), sb("b2_sb", [128, H2 // 128])
        dense_sb = sb("dense_sb", [F_DENSE, B])
        mask = sb("mask", [128, TB])
        ident = sb("ident", [M, M])
        idx = sb("idx", [LB, M], i32)
        rows = sb("rows", [LB, M * D])
        x = sb("x", [M, GN])
        xa = sb("xa", [PR, GN])
        pairs = sb("pairs", [PR, NP, GN])
        x1_hi, x1_lo = sb("x1_hi", [O, GN], f32r), sb("x1_lo", [O, GN], f32r)
        x0t = sb("x0t", [128, NT, M])
        acc = sb("acc", [128, 2, MC, O])
        terms = sb("terms", [128, 2, NS, MC * O])
        total = sb("total", [128, MC, O])
        x2 = sb("x2", [128, O])
        x2_hi, x2_lo = sb("x2_hi", [128, 2, O], f32r), sb("x2_lo", [128, 2, O], f32r)
        x0t_parts = sb("x0t_parts", [128, 2, NT, M], f32r)
        blocks = sb("blocks", [128, 2, NT, TB, M1], f32r)
        gram = sb("gram", [O, M1, QB])
        z0 = sb("z0", [O, B])
        z2 = sb("z2", [O, QB])
        h1, h2 = sb("h1", [128, H1 // 128, QB]), sb("h2", [128, H2 // 128, QB])
        y_sb = sb("y_sb", [1, B])
        raw = gram[:, :, :].rearrange("h m b -> h (m b)")
        k1_raw = raw[:, 0:M * O]
        w0_raw = raw[0:PR, M * O:M * O + NP * O]

        y_ps = [bank(f"y_ps{i}") for i in range(YB)]
        xt_ps = bank("xt_ps")
        x1_ps = bank("x1_ps")
        gram_ps = bank("gram_ps")

        ids_loaded, gathered, rows_stored = sem("ids_loaded"), sem("gathered"), sem("rows_stored")
        x_loaded, xa_loaded = sem("x_loaded"), sem("xa_loaded")
        rot_loaded = [sem(f"rot_loaded{c}") for c in range(NP)]
        blocks_loaded, out_stored = sem("blocks_loaded"), sem("out_stored")
        k1_loaded, w0_loaded, small_loaded, late_loaded = (sem("k1_loaded"), sem("w0_loaded"), sem("small_loaded"),
                                                           sem("late_loaded"))
        k1_hi_ready, k1_lo_ready, w0_ready = sem("k1_hi_ready"), sem("k1_lo_ready"), sem("w0_ready")
        blocks_zeroed, blocks_set = sem("blocks_zeroed"), sem("blocks_set")
        pairs_ready = sem("pairs_ready")
        x1_made = sem("x1_made")
        x1_hi_ready, x1_lo_ready, z0_ready = sem("x1_hi_ready"), sem("x1_lo_ready"), sem("z0_ready")
        x0t_made = sem("x0t_made")
        x0t_ready, x0t_hi_ready, x0t_lo_ready = sem("x0t_ready"), sem("x0t_hi_ready"), sem("x0t_lo_ready")
        y_made = sem("y_made")
        y_used_vec = sem("y_used_vec")
        y_used_sca = sem("y_used_sca")
        terms_added = sem("terms_added")
        last_added = sem("last_added")
        terms_used = sem("terms_used")
        x2_summed = sem("x2_summed")
        x2_hi_ready = sem("x2_hi_ready")
        x2_ready = sem("x2_ready")
        gram_made, gram_kept = sem("gram_made"), sem("gram_kept")
        z2_made, z2_ready = sem("z2_made"), sem("z2_ready")
        h1_made, h1_ready = sem("h1_made"), sem("h1_ready")
        h2_made, h2_ready = sem("h2_made"), sem("h2_ready")
        y_out_made, y_out_ready = sem("y_out_made"), sem("y_out_ready")

        def after_first(g):
            return not isinstance(g, int) or g > 0

        block = ctx.enter_context(nc.Block())

        @block.sync
        def _(sp):
            def load_ids(t):
                sp.dma_start(idx[:, :], ids[ds(t * LB, LB), :]).then_inc(ids_loaded, 16)

            def load_x0(g, t=None):
                sp.wait_ge(x0t_made, g + 1)
                sp.wait_ge(x1_made, g + 1)
                if t is not None:
                    sp.wait_ge(rows_stored, t * 32 + 32)
                at = ds(g * GB, GB)
                row = x0_rows[0:M, at, :].rearrange("m b d -> m (b d)")
                sp.dma_start(xa[:, :], row.unsqueeze(1).to_broadcast([M, RC, GN])).then_inc(xa_loaded, 16)
                for c in range(NP):
                    r = x0_rows[RC * c:RC * c + M, at, :].rearrange("m b d -> m (b d)")
                    windows = bass.AP(r.tensor, r.offset, [r.ap[0], [r.ap[0][0], RC], r.ap[1]],
                                      runtime_checks=r.runtime_checks)
                    sp.dma_start(pairs[:, c, :], windows).then_inc(rot_loaded[c], 16)
                sp.dma_start(x[:, :], row).then_inc(x_loaded, 16)

            def load_blocks(g):
                sp.wait_ge(x0t_hi_ready, g + 1)
                sp.wait_ge(x0t_lo_ready, g + 1)
                sp.wait_ge(gram_made, g * NT + FREE)
                for b in range(TB):
                    n = slice(b * D, (b + 1) * D)
                    sp.dma_start(blocks[n, :, :, b, 0:M].rearrange("n s j m -> n (s j) m").bitcast(f32),
                                 x0t_parts[n].rearrange("n s j m -> n (s j) m").bitcast(f32)).then_inc(blocks_loaded, 16)

            def store_rows(t, more):
                sp.wait_ge(gathered, t * (M * 16) + M * 16)
                looked_up = rows[:, :].rearrange("b (m d) -> b m d", m=M)
                at = ds(t * LB, LB)
                sp.dma_start(x0_rows[0:M, at, :].rearrange("m b d -> b m d"), looked_up).then_inc(rows_stored, 16)
                sp.dma_start(x0_rows[M:M + WRAP, at, :].rearrange("m b d -> b m d"),
                             looked_up[:, 0:WRAP]).then_inc(rows_stored, 16)
                if more:
                    load_ids(t + 1)

            def lookup_block(t, more, more_ids):
                for i in range(LG):
                    g = t * LG + i
                    if more and i == LG - 1:
                        store_rows(t + 1, more_ids)
                    if i < LG - 1:
                        load_x0(g + 1)
                    elif more:
                        load_x0(g + 1, t + 1)
                    load_blocks(g)

            load_ids(0)
            sp.dma_start(w0[:, :, :], k0_pairs).then_inc(w0_loaded, 16)
            sp.dma_start(w0_raw, k0_swapped.rearrange("p c o -> p (c o)")).then_inc(w0_loaded, 16)
            sp.dma_start(mask[:, :], block_mask).then_inc(small_loaded, 16)
            sp.dma_start(ident[:, :], identity).then_inc(small_loaded, 16)
            sp.dma_start(k1_raw, k1_t).then_inc(k1_loaded, 16)
            sp.dma_start(k2_sb[:, :, :], k2_t).then_inc(late_loaded, 16)
            sp.dma_start(w1_sb[:, :, :], w1_z).then_inc(late_loaded, 16)
            sp.dma_start(w1d_sb[:, :], w1_dense).then_inc(late_loaded, 16)
            sp.dma_start(w2_sb[:, :, :], w2).then_inc(late_loaded, 16)
            sp.dma_start(w3_sb[:, :], w3).then_inc(late_loaded, 16)
            sp.dma_start(b1_sb[:, :], b1).then_inc(late_loaded, 16)
            sp.dma_start(b2_sb[:, :], b2).then_inc(late_loaded, 16)
            sp.dma_start(dense_sb[:, :], dense_t).then_inc(late_loaded, 16)
            sp.wait_ge(blocks_set, 1)
            store_rows(0, True)
            load_x0(0, 0)
            with sp.Fori(0, NL - 2) as t:
                lookup_block(t, True, True)
            lookup_block(NL - 2, True, False)
            lookup_block(NL - 1, False, False)
            sp.wait_ge(y_out_ready, NQ)
            sp.dma_start(out, y_sb[:, :]).then_inc(out_stored, 16)
            sp.wait_ge(out_stored, 16)

        @block.gpsimd
        def _(pool):
            def gather(m):
                nc.gpsimd.indirect_dma_start(
                    rows[:, m * D:(m + 1) * D], None, tables[m],
                    bass.IndirectOffsetOnAxis(ap=idx[:, m:m + 1], axis=0)).then_inc(gathered, 16)

            def tile(g, j, lookups, next_block=None):
                n, p = NA[j], j % 2
                before = n if next_block is None and j == 0 else 0
                steps = n - 2 if next_block is not None else n
                for m in lookups if before else ():
                    gather(m)
                for i in range(n):
                    if i == 2 and next_block is not None:
                        pool.wait_ge(ids_loaded, next_block * 16 + 16)
                        pool.wait_ge(rows_stored, next_block * 32)
                    if i > 0:
                        pool.wait_ge(terms_added, g * sum(NA) + sum(NA[:j]) + i)
                    pool.wait_ge(y_used_sca, (g * NT + j) * NS + FREE + i + 2)
                    nc.gpsimd.tensor_tensor(terms[:, p, 0], terms[:, p, 0], terms[:, p, i + 1],
                                            ALU.add).then_inc(terms_added, 1)
                    k = i - (n - steps)
                    if not before and k >= 0:
                        for m in lookups[len(lookups) * k // steps:len(lookups) * (k + 1) // steps]:
                            gather(m)

            def groups(g0, n, lookups=(), next_block=None):
                for i in range(n * NT):
                    now = list(range(sum(lookups[:i]), sum(lookups[:i + 1])))
                    tile(g0 + i // NT, i % NT, now, next_block if i == 0 else None)

            nc.gpsimd.memset(blocks[:, :, :, :, :].rearrange("n s j b m -> n (s j b m)").bitcast(f32),
                             0.0).then_inc(blocks_zeroed, 1)
            pool.wait_ge(ids_loaded, 16)
            for m in range(M):
                gather(m)
            pool.wait_ge(small_loaded, 32)
            pool.wait_ge(blocks_zeroed, 1)
            nc.gpsimd.tensor_copy(blocks[:, 0, :, :, M:M1],
                                  mask[:, :].unsqueeze(1).unsqueeze(3).to_broadcast([128, NT, TB, 1])
                                  ).then_inc(blocks_set, 1)
            groups(0, LG - 1, LOOKUPS_3, 1)
            with pool.Fori(0, NL - 2) as t:
                groups(t * LG + (LG - 1), LG, LOOKUPS_4, t + 2)
            groups((NL - 1) * LG - 1, LG + 1)

        @block.tensor
        def _(pe):
            def first_layer(g, c0, c1):
                for c in range(c0, c1):
                    if c == 0 and after_first(g):
                        pe.wait_ge(z0_ready, g)
                    pe.wait_ge(pairs_ready, g * NP + c + 1)
                    ins = nc.tensor.matmul(x1_ps[:, :], w0[:, c, :], pairs[:, c, :], start=c == 0, stop=c == NP - 1)
                if c1 == NP:
                    ins.then_inc(x1_made, 1)

            def wait_x0(g):
                pe.wait_ge(x_loaded, g * 16 + 16)
                if after_first(g):
                    pe.wait_ge(x0t_ready, g)
                    pe.wait_ge(x0t_hi_ready, g)

            def transpose_x0(g):
                for j in range(NT):
                    ins = nc.tensor.transpose(xt_ps[:, j * M:(j + 1) * M], x[:, j * 128:(j + 1) * 128], ident[:, :])
                ins.then_inc(x0t_made, 1)

            def second_layer(g, j, c):
                s = j * NC + c
                if s in (0, NC):
                    pe.wait_ge(x1_hi_ready, 2 * g + 1 + (s > 0))
                mine, before = (VEC, y_used_vec) if (s - YB) % NC in VEC else (SCA, y_used_sca)
                pe.wait_ge(before, g * (NT * len(mine)) + taken(mine, s - YB + 1) + FREE)
                ps, n, k = y_ps[s % YB], slice(j * 128, (j + 1) * 128), slice(c * MC * O, (c + 1) * MC * O)
                nc.tensor.matmul(ps[:, :], x1_hi[:, n], k1_hi[:, k], start=True, stop=False)
                nc.tensor.matmul(ps[:, :], x1_hi[:, n], k1_lo[:, k], start=False, stop=False)
                if s in (0, NC):
                    pe.wait_ge(x1_lo_ready, 2 * g + 1 + (s > 0))
                nc.tensor.matmul(ps[:, :], x1_lo[:, n], k1_hi[:, k], start=False, stop=True).then_inc(y_made, 1)

            def gram_of_tile(g, j):
                k, p = g * NT + j, j % 2
                if j == 0:
                    pe.wait_ge(blocks_loaded, g * (TB * 16) + TB * 16)
                pe.wait_ge(gram_kept, k + FREE)
                pe.wait_ge(x2_ready, k + 1 + FREE)
                for n, (left, part) in enumerate(((x2_hi, 0), (x2_hi, 1), (x2_lo, 0))):
                    ins = nc.tensor.matmul(gram_ps[:, 0:TB * M1], left[:, p],
                                           blocks[:, part, j].rearrange("n b m -> n (b m)"), start=n == 0, stop=n == 2)
                ins.then_inc(gram_made, 1)

            def group(g, more):
                for j in range(NT):
                    for c in range(NC):
                        if more and (j, c) == (2, NC - 1):
                            wait_x0(g + 1)
                        second_layer(g, j, c)
                        if j > 1 and c == GRAM_AT:
                            gram_of_tile(g, j - 2)
                    if more and j == 2:
                        transpose_x0(g + 1)
                if more:
                    first_layer(g + 1, 0, 3)
                gram_of_tile(g, NT - 2)
                if more:
                    first_layer(g + 1, 3, NP)
                else:
                    first_mlp_parts(NQ - 1)
                gram_of_tile(g, NT - 1)

            h2_ps = [x1_ps, y_ps[4]]

            def first_mlp_parts(q):
                pe.wait_ge(y_used_vec, q * (QG * NT * NV) + QG * NT * NV + FREE)
                pe.wait_ge(y_used_sca, q * (QG * NT * NS) + QG * NT * NS + FREE)
                cols = ds(q * QB, QB)
                for o in range(H1 // 128):
                    f = slice(o * 128, (o + 1) * 128)
                    hp = y_ps[o][:, 0:QB]
                    nc.tensor.matmul(hp, w1_sb[:, 0, f], z0[:, cols], start=True, stop=False)
                    nc.tensor.matmul(hp, w1d_sb[:, f], dense_sb[:, cols], start=False, stop=False)

            def third_layer_and_mlp(q, x1_read):
                pe.wait_ge(gram_kept, q * (QG * NT) + QG * NT + FREE)
                zp = gram_ps[:, 0:QB]
                for m in range(M):
                    ins = nc.tensor.matmul(zp, k2_sb[:, m, :], gram[:, m, :], start=m == 0, stop=m == M - 1)
                ins.then_inc(z2_made, 1)
                for o in range(H1 // 128):
                    nc.tensor.matmul(y_ps[o][:, 0:QB], w1_sb[:, 1, o * 128:(o + 1) * 128], gram[:, M, :],
                                     start=False, stop=False)
                pe.wait_ge(z2_ready, q + 1)
                for o in range(H1 // 128):
                    nc.tensor.matmul(y_ps[o][:, 0:QB], w1_sb[:, 2, o * 128:(o + 1) * 128], z2[:, :],
                                     start=False, stop=True).then_inc(h1_made, 1)
                pe.wait_ge(z0_ready, x1_read)
                for i in range(H1 // 128):
                    pe.wait_ge(h1_ready, q * (H1 // 128) + i + 1)
                    for o in range(H2 // 128):
                        ins = nc.tensor.matmul(h2_ps[o][:, 0:QB], w2_sb[:, i, o * 128:(o + 1) * 128], h1[:, i, :],
                                               start=i == 0, stop=i == H1 // 128 - 1)
                        if i == H1 // 128 - 1:
                            ins.then_inc(h2_made, 1)
                for i in range(H2 // 128):
                    pe.wait_ge(h2_ready, q * (H2 // 128) + i + 1)
                    ins = nc.tensor.matmul(gram_ps[0:1, 0:QB], w3_sb[:, i:i + 1], h2[:, i, :],
                                           start=i == 0, stop=i == H2 // 128 - 1)
                ins.then_inc(y_out_made, 1)
                pe.wait_ge(y_out_ready, q + 1)

            pe.sem_inc(x0t_made, 1)
            pe.sem_inc(x1_made, 1)
            pe.sem_inc(gram_made, FREE)
            pe.wait_ge(small_loaded, 32)
            pe.wait_ge(w0_ready, 1)
            first_layer(0, 0, NP)
            wait_x0(0)
            transpose_x0(0)
            pe.wait_ge(k1_hi_ready, 1)
            pe.wait_ge(k1_lo_ready, 1)
            with pe.Fori(0, NQ - 1) as q:
                with pe.Fori(0, QG) as i:
                    group(q * QG + i, True)
                pe.wait_ge(late_loaded, 8 * 16)
                first_mlp_parts(q)
                third_layer_and_mlp(q, q * QG + QG + 1)
            with pe.Fori(0, QG - 1) as i:
                group(i + (NQ - 1) * QG, True)
            group(NG - 1, False)
            third_layer_and_mlp(NQ - 1, NG)

        @block.scalar
        def _(act):
            def round_x1(g):
                act.wait_ge(x1_lo_ready, 2 * g + 1)
                nc.scalar.activation(x1_hi[:, 128:GN], x1_ps[:, 128:GN], ACT.Copy).then_inc(x1_hi_ready, 1)

            def keep_x0t(g):
                act.wait_ge(x0t_made, g + 2)
                if after_first(g):
                    act.wait_ge(y_used_vec, g * (NT * NV) + FREE)
                    act.wait_ge(y_used_sca, g * (NT * NS) + FREE)
                    act.wait_ge(x0t_lo_ready, g)
                transposed = xt_ps[:, 0:NT * M].rearrange("n (j m) -> n j m", j=NT)
                nc.scalar.activation(x0t[:, :, :], transposed, ACT.Copy).then_inc(x0t_ready, 1)
                if after_first(g):
                    act.wait_ge(blocks_loaded, g * (TB * 16))
                nc.scalar.activation(x0t_parts[:, 0], transposed, ACT.Copy).then_inc(x0t_hi_ready, 1)

            def weight_chunk(g, j, i):
                c, s = SCA[i], j * NC + SCA[i]
                if i == 0:
                    act.wait_ge(terms_used, g * NT + j + FREE - 1)
                act.wait_ge(y_made, g * (NT * NC) + s + 1)
                for r in range(MC):
                    m = c * MC + r
                    ins = nc.scalar.activation(terms[:, j % 2, i, r * O:(r + 1) * O],
                                               y_ps[s % YB][:, r * O:(r + 1) * O], ACT.Copy, scale=x0t[:, j, m:m + 1])
                ins.then_inc(y_used_sca, 1)

            def round_x2(g, j):
                k = g * NT + j
                act.wait_ge(x2_summed, k + 1 + FREE)
                act.wait_ge(gram_made, k + FREE - 1)
                nc.scalar.activation(x2_hi[:, j % 2], x2[:, :], ACT.Copy).then_inc(x2_hi_ready, 1)

            def keep_gram(g, i, j):
                act.wait_ge(gram_made, g * NT + j + 1 + FREE)
                nc.scalar.activation(gram[:, :, ds(i * GB + j * TB, TB)],
                                     gram_ps[:, 0:TB * M1].rearrange("h (b m) -> h m b", b=TB),
                                     ACT.Copy).then_inc(gram_kept, 1)

            def group(g, i, more):
                act.wait_ge(x0t_ready, g + 1)
                for j in range(NT):
                    for n in range(NS):
                        weight_chunk(g, j, n)
                        if j > 1 and n == 4:
                            keep_gram(g, i, j - 2)
                        if j > 0 and n == 4:
                            round_x2(g, j - 1)
                if more:
                    keep_x0t(g + 1)
                keep_gram(g, i, NT - 2)
                round_x2(g, NT - 1)
                if more:
                    round_x1(g + 1)
                keep_gram(g, i, NT - 1)

            def mlp(q):
                act.wait_ge(z2_made, q + 1)
                nc.scalar.activation(z2[:, :], gram_ps[:, 0:QB], ACT.Copy).then_inc(z2_ready, 1)
                for o in range(H1 // 128):
                    act.wait_ge(h1_made, q * (H1 // 128) + o + 1)
                    nc.scalar.activation(h1[:, o, :], y_ps[o][:, 0:QB], ACT.Relu,
                                         bias=b1_sb[:, o:o + 1]).then_inc(h1_ready, 1)
                for o, ps in enumerate((x1_ps, y_ps[4])):
                    act.wait_ge(h2_made, q * (H2 // 128) + o + 1)
                    nc.scalar.activation(h2[:, o, :], ps[:, 0:QB], ACT.Relu,
                                         bias=b2_sb[:, o:o + 1]).then_inc(h2_ready, 1)
                act.wait_ge(y_out_made, q + 1)
                nc.scalar.activation(y_sb[:, ds(q * QB, QB)], gram_ps[0:1, 0:QB], ACT.Copy).then_inc(y_out_ready, 1)

            act.sem_inc(y_used_sca, FREE)
            act.sem_inc(gram_kept, FREE)
            act.wait_ge(k1_loaded, 16)
            nc.scalar.activation(k1_hi[:, :], k1_raw, ACT.Copy).then_inc(k1_hi_ready, 1)
            keep_x0t(0)
            round_x1(0)
            with act.Fori(0, NQ - 1) as q:
                with act.Fori(0, QG) as i:
                    group(q * QG + i, i, True)
                act.wait_ge(late_loaded, 8 * 16)
                mlp(q)
            with act.Fori(0, QG - 1) as i:
                group(i + (NQ - 1) * QG, i, True)
            group(NG - 1, QG - 1, False)
            mlp(NQ - 1)

        @block.vector
        def _(dve):
            def pair_products(g, c):
                if c == 0:
                    dve.wait_ge(xa_loaded, g * 16 + 16)
                dve.wait_ge(rot_loaded[c], g * 16 + 16)
                nc.vector.tensor_tensor(pairs[:, c, :], pairs[:, c, :], xa[:, :], ALU.mult).then_inc(pairs_ready, 1)

            def low_x1(g):
                dve.wait_ge(x1_made, g + 2)
                nc.vector.tensor_copy(x1_hi[:, 0:128], x1_ps[:, 0:128]).then_inc(x1_hi_ready, 1)
                for i, n in enumerate((slice(0, 128), slice(128, GN))):
                    dve.wait_ge(x1_hi_ready, 2 * g + i + 1)
                    nc.vector.tensor_tensor(x1_lo[:, n], x1_ps[:, n], x1_hi[:, n].bitcast(f32),
                                            ALU.subtract).then_inc(x1_lo_ready, 1)
                nc.vector.tensor_reduce(z0[:, ds(g * GB, GB)], x1_ps[:, :].rearrange("o (b d) -> o b d", d=D),
                                        AX.X, ALU.add).then_inc(z0_ready, 1)

            def low_x0t(g):
                dve.wait_ge(x0t_hi_ready, g + 1)
                nc.vector.tensor_tensor(x0t_parts[:, 1], x0t[:, :, :], x0t_parts[:, 0].bitcast(f32),
                                        ALU.subtract).then_inc(x0t_lo_ready, 1)

            def weight_chunk(g, j, i):
                c, p, s = VEC[i], j % 2, j * NC + VEC[i]
                y = y_ps[s % YB]
                if i > 0:
                    dve.wait_ge(y_used_vec, g * (NT * NV) + j * NV + i + FREE)
                else:
                    dve.wait_ge(terms_used, g * NT + j + FREE - 1)
                dve.wait_ge(y_made, g * (NT * NC) + s + 1)
                if i == 0:
                    nc.vector.tensor_tensor(acc[:, p], y[:, :].rearrange("n (m o) -> n m o", m=MC),
                                            x0t[:, j, c * MC:(c + 1) * MC].unsqueeze(2).to_broadcast([128, MC, O]),
                                            ALU.mult).then_inc(y_used_vec, 1)
                    return
                for r in range(MC):
                    m = c * MC + r
                    ins = nc.vector.scalar_tensor_tensor(acc[:, p, r], y[:, r * O:(r + 1) * O], x0t[:, j, m:m + 1],
                                                         acc[:, p, r], ALU.mult, ALU.add)
                ins.then_inc(y_used_vec, 1)

            flat = total[:, :, :].rearrange("n r o -> n (r o)")

            def add_last_terms(g, j):
                k, p = g * NT + j, j % 2
                dve.wait_ge(y_used_vec, k * NV + NV + FREE)
                dve.wait_ge(y_used_sca, k * NS + NS + FREE)
                dve.wait_ge(x2_summed, k + FREE)
                sum_so_far = acc[:, p].rearrange("n r o -> n (r o)")
                for n, i in enumerate(reversed(range(NA[j] + 1, NS))):
                    if n > 0:
                        dve.wait_ge(last_added, g * LAST + sum(NS - 1 - a for a in NA[:j]) + n)
                    nc.vector.tensor_tensor(flat, sum_so_far, terms[:, p, i], ALU.add).then_inc(last_added, 1)
                    sum_so_far = flat

            def add_terms(g, j):
                k, p = g * NT + j, j % 2
                dve.wait_ge(last_added, g * LAST + sum(NS - 1 - a for a in NA[:j + 1]))
                dve.wait_ge(terms_added, g * sum(NA) + sum(NA[:j + 1]))
                nc.vector.tensor_tensor(flat, flat, terms[:, p, 0], ALU.add).then_inc(terms_used, 1)

            def sum_total(g, j):
                k = g * NT + j
                dve.wait_ge(terms_used, k + 1 + FREE)
                dve.wait_ge(x2_ready, k + FREE)
                nc.vector.tensor_reduce(x2[:, :], total[:, :, :].rearrange("n r o -> n o r"), AX.X,
                                        ALU.add).then_inc(x2_summed, 1)

            def low_x2(g, j):
                k, p = g * NT + j, j % 2
                dve.wait_ge(x2_hi_ready, k + 1)
                nc.vector.tensor_tensor(x2_lo[:, p], x2[:, :], x2_hi[:, p].bitcast(f32),
                                        ALU.subtract).then_inc(x2_ready, 1)

            finish = [add_last_terms, add_terms, sum_total, low_x2]

            def group(g, more):
                dve.wait_ge(x0t_ready, g + 1)
                for j in range(NT):
                    for n in range(NV):
                        weight_chunk(g, j, n)
                        if j > 0:
                            finish[n](g, j - 1)
                        if more and (j, n) in PAIR_SLOTS:
                            pair_products(g + 1, PAIR_SLOTS.index((j, n)))
                for step in finish:
                    step(g, NT - 1)
                if more:
                    low_x1(g + 1)
                    low_x0t(g + 1)

            for free in (y_used_vec, terms_used, x2_summed, x2_ready):
                dve.sem_inc(free, FREE)
            dve.wait_ge(w0_loaded, 32)
            nc.vector.tensor_tensor(w0[:, :, :].rearrange("p c o -> p (c o)"),
                                    w0[:, :, :].rearrange("p c o -> p (c o)"), w0_raw, ALU.add).then_inc(w0_ready, 1)
            dve.wait_ge(k1_hi_ready, 1)
            nc.vector.tensor_tensor(k1_lo[:, :], k1_raw, k1_hi[:, :].bitcast(f32), ALU.subtract
                                    ).then_inc(k1_lo_ready, 1)
            for c in range(NP):
                pair_products(0, c)
            low_x1(0)
            dve.wait_ge(x0t_ready, 1)
            low_x0t(0)
            with dve.Fori(0, NG - 1) as g:
                group(g, True)
            group(NG - 1, False)


def kernel(**inputs):
    import numpy as np
    import concourse.bacc as bacc
    from concourse.bass_utils import run_bass_kernel_spmd

    def host(name):
        return np.ascontiguousarray(inputs[name])

    k0 = host("L0_rec_k0")
    h = np.arange(M)
    k0_pairs = np.zeros((M, RC, NP, O), k0.dtype)
    k0_swapped = np.zeros((M, RC, NP, O), k0.dtype)
    for a in range(RC):
        for c in range(NP):
            r = RC * c + a
            m = (h + r) % M
            k0_pairs[:, a, c] = k0[:, h, m].T
            if 0 < r < M // 2:
                k0_swapped[:, a, c] = k0[:, m, h].T
    block_mask = np.repeat(np.eye(TB, dtype=np.float32), D, axis=0)

    w1 = host("W_top1")
    arrays = {
        "ids": host("ids"),
        "dense_t": host("dense_ctx").T,
        "k0_pairs": k0_pairs.reshape(PR, NP, O),
        "k0_swapped": k0_swapped.reshape(PR, NP, O),
        "k1_t": host("L0_rec_k1").transpose(1, 2, 0).reshape(O, M * O),
        "k2_t": host("L0_rec_k2").transpose(1, 2, 0),
        "w1_z": w1[:3 * O].reshape(3, O, H1).transpose(1, 0, 2),
        "w1_dense": w1[3 * O:],
        "b1": host("b_top1").reshape(H1 // 128, 128).T,
        "w2": host("W_top2").reshape(H1 // 128, 128, H2).transpose(1, 0, 2),
        "b2": host("b_top2").reshape(H2 // 128, 128).T,
        "w3": host("W_top3").reshape(H2 // 128, 128).T,
        "block_mask": block_mask,
        "identity": np.eye(M, dtype=np.float32),
    }
    for m in range(M):
        arrays[f"tbl_{m}"] = host(f"tbl_{m}")
    arrays = {f"in_{k}": np.ascontiguousarray(v) for k, v in arrays.items()}

    nc = bacc.Bacc("TRN2", target_bir_lowering=False, num_devices=1)
    aps = {k[3:]: nc.dram_tensor(k, v.shape, mybir.dt.from_np(v.dtype), kind="ExternalInput").ap()
           for k, v in arrays.items()}
    tables = [aps.pop(f"tbl_{m}") for m in range(M)]
    out = nc.dram_tensor("out", (1, B), mybir.dt.float32, kind="ExternalOutput").ap()
    cin_tower(nc, tables=tables, out=out, **aps)
    result = run_bass_kernel_spmd(nc, [arrays], core_ids=[0])
    return result.results[0]["out"].reshape(B, 1)
```

```python
from contextlib import ExitStack

import concourse.bass as bass
from concourse import mybir

B, M, D, O = 1024, 40, 16, 128
F_DENSE, H1, H2 = 16, 512, 256
GB = 32
GN = GB * D
NG = B // GB
TB = 128 // D
NT = GB // TB
QB = 256
QG = QB // GB
NQ = B // QB
LP = 128 // GB
LM = M // LP
MC = 4
NC = M // MC
ROT = M // 2 + 1
RC = 3
NP = ROT // RC
PR = RC * M
WRAP = ROT - 1
M1 = M + 1

KINDS = "VPPVPVPPVA"
SLOTS = KINDS * NT
NY = len(SLOTS)
VEC = [s for s in range(NY) if SLOTS[s] == "V"]
SCA = [s for s in range(NY) if SLOTS[s] in "AP"]
NV, NS = len(VEC), len(SCA)


def slots_of(kind, j):
    return [j * NC + c for c in range(NC) if KINDS[c] == kind]


NSUM = 2 + KINDS.count("A")
NA = KINDS.count("P") - 1


def place(s):
    c = s % NC
    if KINDS[c] == "A":
        return 2 + KINDS[:c].count("A")
    n = KINDS[:c].count("P")
    return 1 if n == 0 else NSUM + n - 1


YB = 5
PAIR_SLOTS = [3, 8, 10, 13, 18, 20, 25]
XA_SLOT = 1
SPLIT = [3, 4, 5]
HI_SLOTS, LO_SLOTS = [16, 19, 22], [20, 23, 28]
P_SLOTS = [9, 13, 17, 24, 28, 32, 30]
X1_SLOTS_VEC, X1_SLOT_SCA = (33, 38), 36
MLP_TILE = 1
SUM_AT, LOW_AT, ROUND_AT = 5, 8, 7
GRAM_AT = 4
X0T_TILE = 3
X0T_AT = TB * (M + 1)
LOOKUPS = [2, 4, 4]
FREE = 4


def cin_tower(nc, ids, table_starts, tables, dense_t, k0_pairs, k0_swapped, k1_t, k2_t, w1_z, w1_dense, b1,
              w2, b2, w3, block_mask, identity, out):
    f32, f32r, i32 = mybir.dt.float32, mybir.dt.float32r, mybir.dt.int32
    ALU, ACT, AX = mybir.AluOpType, mybir.ActivationFunctionType, mybir.AxisListType
    ds = bass.ds

    x0_rows = nc.dram_tensor("x0_rows", (M + WRAP, B, D), f32, kind="Internal").ap()

    with ExitStack() as ctx:
        def sb(name, shape, dt=f32):
            return ctx.enter_context(nc.sbuf_tensor(name, shape, dt))

        def bank(name):
            return ctx.enter_context(nc.psum_tensor(name, [128, 512], f32))

        def sem(name):
            return ctx.enter_context(nc.semaphore(name))

        k1_hi, k1_lo = sb("k1_hi", [O, M * O], f32r), sb("k1_lo", [O, M * O], f32r)
        k2_sb = sb("k2_sb", [O, M, O])
        w0 = sb("w0", [PR, NP, O])
        w0_parts = sb("w0_parts", [PR, 2, len(SPLIT), O], f32r)
        w1_sb, w1d_sb = sb("w1_sb", [O, 3, H1]), sb("w1d_sb", [F_DENSE, H1])
        w2_sb, w3_sb = sb("w2_sb", [128, H1 // 128, H2]), sb("w3_sb", [128, H2 // 128])
        b1_sb, b2_sb = sb("b1_sb", [128, H1 // 128]), sb("b2_sb", [128, H2 // 128])
        dense_sb = sb("dense_sb", [F_DENSE, QB])
        mask = sb("mask", [128, TB])
        ident = sb("ident", [M, M])
        starts = sb("starts", [128, LM], i32)
        ids_sb, idx = sb("ids_sb", [128, 2, LM], i32), sb("idx", [128, 2, LM], i32)
        rows = sb("rows", [128, 2, LM, D])
        x = sb("x", [M, GN])
        xa = sb("xa", [PR, GN])
        pairs = sb("pairs", [PR, NP, GN])
        split_hi, split_lo = sb("split_hi", [PR, len(SPLIT), GN], f32r), sb("split_lo", [PR, len(SPLIT), GN], f32r)
        x1_hi, x1_lo = sb("x1_hi", [O, 2, GN], f32r), sb("x1_lo", [O, 2, GN], f32r)
        x0t = sb("x0t", [128, 2, NT, M])
        sums = sb("sums", [128, 2, NSUM + NA, MC * O])
        x2 = sb("x2", [128, O])
        x2_hi, x2_lo = sb("x2_hi", [128, 2, O], f32r), sb("x2_lo", [128, 2, O], f32r)
        x0t_parts = sb("x0t_parts", [128, NT, 2, M], f32r)
        blocks = sb("blocks", [128, NT, 2, TB, M1], f32r)
        gram = sb("gram", [O, M1, QB])
        z0 = sb("z0", [O, B])
        h1, h2 = gram[:, 0:H1 // 128, :], gram[:, H1 // 128:(H1 + H2) // 128, :]
        z2 = gram[:, (H1 + H2) // 128, :]
        y_sb = z0[0:1, :]
        raw = gram[:, :, :].rearrange("h m b -> h (m b)")
        k1_raw = raw[:, 0:M * O]
        w0_raw = raw[0:PR, M * O:M * O + NP * O]

        y_ps = [bank(f"y_ps{i}") for i in range(YB)]
        xa_ps = bank("xa_ps")
        x1_ps = bank("x1_ps")
        gram_ps = bank("gram_ps")

        starts_loaded, idx_ready = sem("starts_loaded"), sem("idx_ready")
        ids_loaded = [sem(f"ids_loaded{e}") for e in range(2)]
        gathered = [sem(f"gathered{e}") for e in range(2)]
        rows_stored = [sem(f"rows_stored{e}") for e in range(2)]
        x_loaded, xa_loaded = sem("x_loaded"), sem("xa_loaded")
        rot_loaded = [sem(f"rot_loaded{c}") for c in range(NP)]
        blocks_loaded = [sem(f"blocks_loaded{h}") for h in range(2)]
        dense_loaded, out_stored = sem("dense_loaded"), sem("out_stored")
        k1_loaded, w0_loaded, small_loaded, late_loaded = (sem("k1_loaded"), sem("w0_loaded"), sem("small_loaded"),
                                                           sem("late_loaded"))
        k1_hi_ready, k1_lo_ready, w0_ready = sem("k1_hi_ready"), sem("k1_lo_ready"), sem("w0_ready")
        w0_hi_ready, w0_lo_ready = sem("w0_hi_ready"), sem("w0_lo_ready")
        blocks_zeroed, blocks_set = sem("blocks_zeroed"), sem("blocks_set")
        xa_kept = sem("xa_kept")
        pairs_ready = sem("pairs_ready")
        split_hi_ready, split_lo_ready = sem("split_hi_ready"), sem("split_lo_ready")
        x1_made = sem("x1_made")
        x1_hi_ready, x1_lo_ready, z0_ready = sem("x1_hi_ready"), sem("x1_lo_ready"), sem("z0_ready")
        x0t_made = sem("x0t_made")
        x0t_ready, x0t_hi_ready, x0t_lo_ready = sem("x0t_ready"), sem("x0t_hi_ready"), sem("x0t_lo_ready")
        y_made = sem("y_made")
        y_used_vec = sem("y_used_vec")
        y_used_sca = sem("y_used_sca")
        terms_added = sem("terms_added")
        x2_summed = sem("x2_summed")
        x2_hi_ready = sem("x2_hi_ready")
        x2_ready = sem("x2_ready")
        gram_made, gram_kept = sem("gram_made"), sem("gram_kept")
        z2_made, z2_ready = sem("z2_made"), sem("z2_ready")
        h1_made, h1_ready = sem("h1_made"), sem("h1_ready")
        h2_made, h2_ready = sem("h2_made"), sem("h2_ready")
        y_out_made, y_out_ready = sem("y_out_made"), sem("y_out_ready")

        STORES = LP + WRAP // LM

        def dmas(even, n):
            return even * (n * 8) + n * 16

        def after_first(g):
            return not isinstance(g, int) or g > 0

        def all_pairs(engine, pair):
            pair(0, 0)
            with engine.Fori(0, QG // 2 - 1) as p:
                pair(p * 2 + 2, p * 2 + 2)
            with engine.Fori(0, NQ - 2) as q:
                pair(q * QG + QG, 0, q)
                with engine.Fori(0, QG // 2 - 1) as p:
                    pair(q * QG + QG + p * 2 + 2, p * 2 + 2)
            pair(NG - QG, 0, NQ - 2)
            with engine.Fori(0, QG // 2 - 2) as p:
                pair(NG - QG + p * 2 + 2, p * 2 + 2)
            pair(NG - 2, QG - 2)

        block = ctx.enter_context(nc.Block())

        @block.sync
        def _(sp):
            def load_ids(even, e):
                if after_first(even):
                    sp.wait_ge(idx_ready, even + e - 1)
                sp.dma_start(ids_sb[:, e], ids[ds(even + e, 1)].rearrange("g p k -> (g p) k")
                             ).then_inc(ids_loaded[e], 16)

            def load_x0(even, e):
                g = even + e
                sp.wait_ge(x0t_made, g + 1)
                sp.wait_ge(x1_made, g + 1)
                sp.wait_ge(rows_stored[e], dmas(even, STORES))
                at = ds(g * GB, GB)
                row = x0_rows[0:M, at, :].rearrange("m b d -> m (b d)")
                sp.dma_start(xa[:, :], row.unsqueeze(1).to_broadcast([M, RC, GN])).then_inc(xa_loaded, 16)
                for c in range(NP):
                    r = x0_rows[RC * c:RC * c + M, at, :].rearrange("m b d -> m (b d)")
                    windows = bass.AP(r.tensor, r.offset, [r.ap[0], [r.ap[0][0], RC], r.ap[1]],
                                      runtime_checks=r.runtime_checks)
                    sp.dma_start(pairs[:, c, :], windows).then_inc(rot_loaded[c], 16)
                sp.dma_start(x[:, :], row).then_inc(x_loaded, 16)

            def load_blocks(g, h):
                if h == 0:
                    sp.wait_ge(x0t_hi_ready, g + 1)
                    sp.wait_ge(x0t_lo_ready, g + 1)
                sp.wait_ge(gram_made, g * NT + (FREE - 2 + 2 * h))
                j = slice(2 * h, 2 * h + 2)
                for b in range(TB):
                    n = slice(b * D, (b + 1) * D)
                    sp.dma_start(blocks[n, j, :, b, 0:M].rearrange("n j s m -> n (j s) m").bitcast(f32),
                                 x0t_parts[n, j].rearrange("n j s m -> n (j s) m").bitcast(f32)
                                 ).then_inc(blocks_loaded[h], 16)

            def store_rows(even, e):
                sp.wait_ge(gathered[e], dmas(even, LM))
                at = ds((even + e) * GB, GB)
                for first in (0, M):
                    for part in range(LP if first == 0 else WRAP // LM):
                        m = first + part * LM
                        sp.dma_start(x0_rows[m:m + LM, at, :].rearrange("m b d -> b m d"),
                                     rows[part * GB:(part + 1) * GB, e]).then_inc(rows_stored[e], 16)

            def group_loads(even, e, ids_later=True, later=True, next_group=True):
                g = even + e
                if ids_later:
                    load_ids(even + 2 + 2 * e, 1 - e)
                load_blocks(g, 1)
                if later:
                    store_rows(even + 2, e)
                    load_x0(even + 2, e)
                if next_group:
                    load_blocks(g + 1, 0)

            load_ids(0, 0)
            sp.dma_start(starts[:, :], table_starts).then_inc(starts_loaded, 16)
            load_ids(0, 1)
            sp.dma_start(w0[:, :, :], k0_pairs).then_inc(w0_loaded, 16)
            sp.dma_start(w0_raw, k0_swapped.rearrange("p c o -> p (c o)")).then_inc(w0_loaded, 16)
            sp.dma_start(mask[:, :], block_mask).then_inc(small_loaded, 16)
            sp.dma_start(ident[:, :], identity).then_inc(small_loaded, 16)
            sp.dma_start(k1_raw, k1_t).then_inc(k1_loaded, 16)
            store_rows(0, 0)
            load_x0(0, 0)
            load_ids(2, 0)
            store_rows(0, 1)
            load_x0(0, 1)
            sp.dma_start(k2_sb[:, :, :], k2_t).then_inc(late_loaded, 16)
            sp.dma_start(w1_sb[:, :, :], w1_z).then_inc(late_loaded, 16)
            sp.dma_start(w1d_sb[:, :], w1_dense).then_inc(late_loaded, 16)
            sp.dma_start(w2_sb[:, :, :], w2).then_inc(late_loaded, 16)
            sp.dma_start(w3_sb[:, :], w3).then_inc(late_loaded, 16)
            sp.dma_start(b1_sb[:, :], b1).then_inc(late_loaded, 16)
            sp.dma_start(b2_sb[:, :], b2).then_inc(late_loaded, 16)
            sp.dma_start(dense_sb[:, :], dense_t[:, 0:QB]).then_inc(dense_loaded, 16)
            sp.wait_ge(blocks_set, 1)
            load_blocks(0, 0)
            with sp.Fori(0, NG // 2 - 2) as p:
                group_loads(p * 2, 0)
                group_loads(p * 2, 1)
            group_loads(NG - 4, 0)
            group_loads(NG - 4, 1, False)
            group_loads(NG - 2, 0, False, False)
            group_loads(NG - 2, 1, False, False, False)
            sp.wait_ge(y_out_ready, NQ)
            sp.dma_start(out, y_sb[:, :]).then_inc(out_stored, 16)
            sp.wait_ge(out_stored, 16)

        @block.gpsimd
        def _(pool):
            def set_idx(even, e):
                pool.wait_ge(ids_loaded[e], dmas(even, 1))
                if after_first(even):
                    pool.wait_ge(gathered[e], dmas(even - 2, LM))
                nc.gpsimd.tensor_tensor(idx[:, e], ids_sb[:, e], starts[:, :], ALU.add).then_inc(idx_ready, 1)

            def wait_idx(even, e):
                pool.wait_ge(idx_ready, even + e + 1)
                if after_first(even):
                    pool.wait_ge(rows_stored[e], dmas(even - 2, STORES))

            def gather(e, k):
                nc.gpsimd.indirect_dma_start(
                    rows[:, e, k], None, tables,
                    bass.IndirectOffsetOnAxis(ap=idx[:, e, k:k + 1], axis=0)).then_inc(gathered[e], 16)

            def group(even, e, later=True, ahead=True):
                g, third = even + e, (even + 2 + 2 * e, 1 - e)
                for j in range(NT):
                    p = j % 2
                    lookups = range(sum(LOOKUPS[:j + 1]), sum(LOOKUPS[:j + 2])) if later else ()
                    for i in range(NA):
                        if ahead and j == NT - 1 and i == NA - 2:
                            set_idx(*third)
                        if ahead and j == NT - 1 and i == NA - 1:
                            wait_idx(*third)
                        if i > 0:
                            pool.wait_ge(terms_added, (g * NT + j) * NA + i)
                        s = slots_of("P", j)[i + 1]
                        pool.wait_ge(y_used_sca, g * NS + SCA.index(s) + 1 + FREE)
                        nc.gpsimd.tensor_tensor(sums[:, p, 1], sums[:, p, 1], sums[:, p, place(s)],
                                                ALU.add).then_inc(terms_added, 1)
                        for k in lookups[len(lookups) * i // NA:len(lookups) * (i + 1) // NA]:
                            gather(e, k)
                if ahead:
                    for k in range(LOOKUPS[0]):
                        gather(third[1], k)

            pool.wait_ge(starts_loaded, 16)
            for e in range(2):
                set_idx(0, e)
            for e in range(2):
                wait_idx(0, e)
                for k in range(LM):
                    gather(e, k)
            nc.gpsimd.memset(blocks[:, :, :, :, :].rearrange("n j s b m -> n (j s b m)").bitcast(f32),
                             0.0).then_inc(blocks_zeroed, 1)
            pool.wait_ge(small_loaded, 32)
            pool.wait_ge(blocks_zeroed, 1)
            nc.gpsimd.tensor_copy(blocks[:, :, 0, :, M:M1],
                                  mask[:, :].unsqueeze(1).unsqueeze(3).to_broadcast([128, NT, TB, 1])
                                  ).then_inc(blocks_set, 1)
            set_idx(2, 0)
            wait_idx(2, 0)
            for k in range(LOOKUPS[0]):
                gather(0, k)
            with pool.Fori(0, NG // 2 - 2) as p:
                group(p * 2, 0)
                group(p * 2, 1)
            group(NG - 4, 0)
            group(NG - 4, 1, True, False)
            group(NG - 2, 0, False, False)
            group(NG - 2, 1, False, False)

        @block.tensor
        def _(pe):
            def first_layer(g, c, first=0, last=SPLIT[-1]):
                if c == first and after_first(g):
                    pe.wait_ge(z0_ready, g)
                if c in SPLIT:
                    n = SPLIT.index(c)
                    pe.wait_ge(split_hi_ready, g * len(SPLIT) + n + 1)
                    passes = [(w0_parts[:, 0, n], split_hi[:, n]), (w0_parts[:, 1, n], split_hi[:, n]),
                              (w0_parts[:, 0, n], split_lo[:, n])]
                else:
                    pe.wait_ge(pairs_ready, g * NP + c + 1)
                    passes = [(w0[:, c, :], pairs[:, c, :])]
                for i, (left, right) in enumerate(passes):
                    if i == 2:
                        pe.wait_ge(split_lo_ready, g * len(SPLIT) + SPLIT.index(c) + 1)
                    ins = nc.tensor.matmul(x1_ps[:, :], left, right, start=c == first and i == 0,
                                           stop=c == last and i == len(passes) - 1)
                if c == last:
                    ins.then_inc(x1_made, 1)

            def transpose_x0():
                for j in range(NT):
                    ins = nc.tensor.transpose(gram_ps[:, X0T_AT + j * M:X0T_AT + (j + 1) * M],
                                              x[:, j * 128:(j + 1) * 128], ident[:, :])
                ins.then_inc(x0t_made, 1)

            def second_layer(g, e, s):
                j, c = divmod(s, NC)
                if s in (0, NC):
                    pe.wait_ge(x1_hi_ready, 2 * g + 1 + (s > 0))
                before = (s - YB) % NY
                mine, used = (VEC, y_used_vec) if SLOTS[before] == "V" else (SCA, y_used_sca)
                last_group = len(mine) if s < YB else 0
                pe.wait_ge(used, g * len(mine) - last_group + mine.index(before) + 1 + FREE)
                ps, n, k = y_ps[s % YB], slice(j * 128, (j + 1) * 128), slice(c * MC * O, (c + 1) * MC * O)
                nc.tensor.matmul(ps[:, :], x1_hi[:, e, n], k1_hi[:, k], start=True, stop=False)
                nc.tensor.matmul(ps[:, :], x1_hi[:, e, n], k1_lo[:, k], start=False, stop=False)
                if s in (0, NC):
                    pe.wait_ge(x1_lo_ready, 2 * g + 1 + (s > 0))
                nc.tensor.matmul(ps[:, :], x1_lo[:, e, n], k1_hi[:, k], start=False, stop=True).then_inc(y_made, 1)

            def gram_of_tile(g, j, x0t_used=True):
                k, p = g * NT + j, j % 2
                if j == 2 and x0t_used:
                    pe.wait_ge(x0t_hi_ready, g + 2)
                if j % 2 == 0:
                    pe.wait_ge(blocks_loaded[j // 2], g * (TB * 16) + TB * 16)
                pe.wait_ge(gram_kept, k + FREE)
                pe.wait_ge(x2_ready, k + 1 + FREE)
                for n, (left, part) in enumerate(((x2_hi, 0), (x2_hi, 1), (x2_lo, 0))):
                    ins = nc.tensor.matmul(gram_ps[:, 0:TB * M1], left[:, p],
                                           blocks[:, j, part].rearrange("n b m -> n (b m)"), start=n == 0, stop=n == 2)
                ins.then_inc(gram_made, 1)

            def group(g, e, mlp=None):
                more = not isinstance(g, int) or g < NG - 1
                for s in range(NY):
                    j, c = divmod(s, NC)
                    second_layer(g, e, s)
                    if c == GRAM_AT:
                        if more and j == X0T_TILE:
                            pe.wait_ge(x_loaded, g * 16 + 32)
                        if mlp is not None and j == MLP_TILE + 1:
                            pe.wait_ge(y_out_ready, mlp + 1)
                        if j > 1:
                            gram_of_tile(g, j - 2)
                        elif after_first(g):
                            gram_of_tile(g - 1, j + 2)
                        if more and j == X0T_TILE:
                            transpose_x0()
                    if mlp is not None and s == (MLP_TILE + 1) * NC - 1:
                        third_layer(mlp)
                        pe.wait_ge(y_used_vec, g * NV + sum(v <= s for v in VEC) + FREE)
                        pe.wait_ge(y_used_sca, g * NS + sum(v <= s for v in SCA) + FREE)
                        first_mlp_parts(mlp)
                        rest_of_mlp(mlp)
                    if more and s in P_SLOTS:
                        first_layer(g + 1, P_SLOTS.index(s))

            def pair(g, i, mlp=None):
                group(g, 0, mlp)
                group(g + 1, 1)
                if not after_first(g):
                    pe.wait_ge(late_loaded, 7 * 16)

            def first_mlp_parts(q):
                cols = ds(q * QB, QB)
                pe.wait_ge(dense_loaded, q * 16 + 16)
                for o in range(H1 // 128):
                    f = slice(o * 128, (o + 1) * 128)
                    hp = y_ps[o][:, 0:QB]
                    nc.tensor.matmul(hp, w1_sb[:, 0, f], z0[:, cols], start=True, stop=False)
                    nc.tensor.matmul(hp, w1d_sb[:, f], dense_sb[:, :], start=False, stop=False)

            def third_layer(q):
                pe.wait_ge(gram_kept, q * (QG * NT) + QG * NT + FREE)
                zp = gram_ps[:, 0:QB]
                for m in range(M):
                    ins = nc.tensor.matmul(zp, k2_sb[:, m, :], gram[:, m, :], start=m == 0, stop=m == M - 1)
                ins.then_inc(z2_made, 1)

            h2_ps = [gram_ps, y_ps[4]]

            def rest_of_mlp(q):
                for o in range(H1 // 128):
                    nc.tensor.matmul(y_ps[o][:, 0:QB], w1_sb[:, 1, o * 128:(o + 1) * 128], gram[:, M, :],
                                     start=False, stop=False)
                pe.wait_ge(z2_ready, q + 1)
                for o in range(H1 // 128):
                    nc.tensor.matmul(y_ps[o][:, 0:QB], w1_sb[:, 2, o * 128:(o + 1) * 128], z2,
                                     start=False, stop=True).then_inc(h1_made, 1)
                for i in range(H1 // 128):
                    pe.wait_ge(h1_ready, q * (H1 // 128) + i + 1)
                    for o in range(H2 // 128):
                        ins = nc.tensor.matmul(h2_ps[o][:, 0:QB], w2_sb[:, i, o * 128:(o + 1) * 128], h1[:, i, :],
                                               start=i == 0, stop=i == H1 // 128 - 1)
                        if i == H1 // 128 - 1:
                            ins.then_inc(h2_made, 1)
                for i in range(H2 // 128):
                    pe.wait_ge(h2_ready, q * (H2 // 128) + i + 1)
                    ins = nc.tensor.matmul(gram_ps[0:1, 0:QB], w3_sb[:, i:i + 1], h2[:, i, :],
                                           start=i == 0, stop=i == H2 // 128 - 1)
                ins.then_inc(y_out_made, 1)

            pe.sem_inc(x0t_made, 1)
            pe.sem_inc(x1_made, 1)
            pe.sem_inc(gram_made, FREE)
            pe.wait_ge(small_loaded, 32)
            pe.wait_ge(w0_ready, 1)
            for c in (c for c in range(NP) if c not in SPLIT):
                first_layer(0, c)
            pe.wait_ge(w0_hi_ready, 1)
            pe.wait_ge(w0_lo_ready, 1)
            for c in SPLIT:
                first_layer(0, c)
            pe.wait_ge(x_loaded, 16)
            transpose_x0()
            pe.wait_ge(k1_hi_ready, 1)
            pe.wait_ge(k1_lo_ready, 1)
            all_pairs(pe, pair)
            gram_of_tile(NG - 1, 2, False)
            pe.wait_ge(y_used_vec, NG * NV + FREE)
            pe.wait_ge(y_used_sca, NG * NS + FREE)
            first_mlp_parts(NQ - 1)
            gram_of_tile(NG - 1, 3)
            third_layer(NQ - 1)
            rest_of_mlp(NQ - 1)

        @block.scalar
        def _(act):
            def round_x1(g, e):
                act.wait_ge(x1_lo_ready, 2 * g + 1)
                nc.scalar.activation(x1_hi[:, e, 128:GN], x1_ps[:, 128:GN], ACT.Copy).then_inc(x1_hi_ready, 1)

            def keep_xa(g):
                act.wait_ge(xa_loaded, g * 16 + 16)
                if after_first(g):
                    act.wait_ge(pairs_ready, g * NP)
                nc.scalar.activation(xa_ps[0:PR, :], xa[:, :], ACT.Copy).then_inc(xa_kept, 1)

            def round_pairs(g, n):
                act.wait_ge(pairs_ready, g * NP + SPLIT[n] + 1)
                nc.scalar.activation(split_hi[:, n], pairs[:, SPLIT[n], :], ACT.Copy).then_inc(split_hi_ready, 1)

            def keep_x0t(g, e):
                act.wait_ge(x0t_made, g + 2)
                if after_first(g):
                    act.wait_ge(y_used_vec, g * NV - NV + FREE)
                    act.wait_ge(x0t_lo_ready, g)
                transposed = gram_ps[:, X0T_AT:X0T_AT + NT * M].rearrange("n (j m) -> n j m", j=NT)
                nc.scalar.activation(x0t[:, e], transposed, ACT.Copy).then_inc(x0t_ready, 1)
                if after_first(g):
                    for h in range(2):
                        act.wait_ge(blocks_loaded[h], g * (TB * 16))
                nc.scalar.activation(x0t_parts[:, :, 0], transposed, ACT.Copy).then_inc(x0t_hi_ready, 1)

            def weight_chunk(g, e, s):
                j, c = divmod(s, NC)
                y = y_ps[s % YB]
                weighted = sums[:, j % 2, place(s)]
                if s == min(slots_of("P", j) + slots_of("A", j)):
                    act.wait_ge(x2_summed, g * NT + j + FREE - 1)
                act.wait_ge(y_made, g * NY + s + 1)
                for r in range(MC):
                    o, m = slice(r * O, (r + 1) * O), c * MC + r
                    ins = nc.scalar.activation(weighted[:, o], y[:, o], ACT.Copy, scale=x0t[:, e, j, m:m + 1])
                ins.then_inc(y_used_sca, 1)

            def round_x2(g, j):
                k = g * NT + j
                act.wait_ge(x2_summed, k + 1 + FREE)
                act.wait_ge(gram_made, k + FREE - 1)
                nc.scalar.activation(x2_hi[:, j % 2], x2[:, :], ACT.Copy).then_inc(x2_hi_ready, 1)

            def keep_gram(g, i, j):
                act.wait_ge(gram_made, g * NT + j + 1 + FREE)
                nc.scalar.activation(gram[:, :, ds(i * GB + j * TB, TB)],
                                     gram_ps[:, 0:TB * M1].rearrange("h (b m) -> h m b", b=TB),
                                     ACT.Copy).then_inc(gram_kept, 1)

            def group(g, i, e, mlp=None):
                more = not isinstance(g, int) or g < NG - 1
                last_i = QG - 1 if isinstance(i, int) and i == 0 else i - 1
                act.wait_ge(x0t_ready, g + 1)
                for s in SCA:
                    j, c = divmod(s, NC)
                    weight_chunk(g, e, s)
                    if more and s == XA_SLOT:
                        keep_xa(g + 1)
                    if more and s in HI_SLOTS:
                        round_pairs(g + 1, HI_SLOTS.index(s))
                    if c == GRAM_AT:
                        if more and j == X0T_TILE:
                            act.wait_ge(x0t_made, g + 3)
                        if j > 1:
                            keep_gram(g, i, j - 2)
                        elif after_first(g):
                            keep_gram(g - 1, last_i, j + 2)
                        if more and j == X0T_TILE:
                            keep_x0t(g + 1, 1 - e)
                    if c == ROUND_AT:
                        if j > 0:
                            round_x2(g, j - 1)
                        elif after_first(g):
                            round_x2(g - 1, NT - 1)
                    if more and s == X1_SLOT_SCA:
                        round_x1(g + 1, 1 - e)
                    if mlp is not None and s == (MLP_TILE + 1) * NC - 1:
                        run_mlp(mlp)

            def pair(g, i, mlp=None):
                group(g, i, 0, mlp)
                group(g + 1, i + 1, 1)
                if not after_first(g):
                    act.wait_ge(late_loaded, 7 * 16)

            def run_mlp(q):
                act.wait_ge(z2_made, q + 1)
                nc.scalar.activation(z2, gram_ps[:, 0:QB], ACT.Copy).then_inc(z2_ready, 1)
                for o in range(H1 // 128):
                    act.wait_ge(h1_made, q * (H1 // 128) + o + 1)
                    nc.scalar.activation(h1[:, o, :], y_ps[o][:, 0:QB], ACT.Relu,
                                         bias=b1_sb[:, o:o + 1]).then_inc(h1_ready, 1)
                if not isinstance(q, int) or q < NQ - 1:
                    nc.scalar.dma_start(dense_sb[:, :], dense_t[:, ds(q * QB + QB, QB)]).then_inc(dense_loaded, 16)
                for o, ps in enumerate((gram_ps, y_ps[4])):
                    act.wait_ge(h2_made, q * (H2 // 128) + o + 1)
                    nc.scalar.activation(h2[:, o, :], ps[:, 0:QB], ACT.Relu,
                                         bias=b2_sb[:, o:o + 1]).then_inc(h2_ready, 1)
                act.wait_ge(y_out_made, q + 1)
                nc.scalar.activation(y_sb[:, ds(q * QB, QB)], gram_ps[0:1, 0:QB], ACT.Copy).then_inc(y_out_ready, 1)

            act.sem_inc(y_used_sca, FREE)
            act.sem_inc(gram_kept, FREE)
            split = slice(SPLIT[0], SPLIT[-1] + 1)
            act.wait_ge(w0_ready, 1)
            nc.scalar.activation(w0_parts[:, 0], w0[:, split], ACT.Copy).then_inc(w0_hi_ready, 1)
            act.wait_ge(k1_loaded, 16)
            nc.scalar.activation(k1_hi[:, :], k1_raw, ACT.Copy).then_inc(k1_hi_ready, 1)
            keep_xa(0)
            for n in range(len(SPLIT)):
                round_pairs(0, n)
            keep_x0t(0, 0)
            round_x1(0, 0)
            all_pairs(act, pair)
            keep_gram(NG - 1, QG - 1, 2)
            round_x2(NG - 1, NT - 1)
            keep_gram(NG - 1, QG - 1, 3)
            run_mlp(NQ - 1)

        @block.vector
        def _(dve):
            def pair_products(g, c):
                if c == 0:
                    dve.wait_ge(xa_kept, g + 1)
                dve.wait_ge(rot_loaded[c], g * 16 + 16)
                nc.vector.tensor_tensor(pairs[:, c, :], pairs[:, c, :], xa_ps[0:PR, :], ALU.mult).then_inc(pairs_ready, 1)

            def low_pairs(g, n):
                dve.wait_ge(split_hi_ready, g * len(SPLIT) + n + 1)
                nc.vector.tensor_tensor(split_lo[:, n], pairs[:, SPLIT[n], :], split_hi[:, n].bitcast(f32),
                                        ALU.subtract).then_inc(split_lo_ready, 1)

            def low_x1(g, e, n):
                dve.wait_ge(x1_hi_ready, 2 * g + 1 + (n.start > 0))
                nc.vector.tensor_tensor(x1_lo[:, e, n], x1_ps[:, n], x1_hi[:, e, n].bitcast(f32),
                                        ALU.subtract).then_inc(x1_lo_ready, 1)

            def split_x1_tile(g, e):
                dve.wait_ge(x1_made, g + 2)
                nc.vector.tensor_copy(x1_hi[:, e, 0:128], x1_ps[:, 0:128]).then_inc(x1_hi_ready, 1)
                low_x1(g, e, slice(0, 128))

            def split_x1_rest(g, e):
                low_x1(g, e, slice(128, GN))
                nc.vector.tensor_reduce(z0[:, ds(g * GB, GB)], x1_ps[:, :].rearrange("o (b d) -> o b d", d=D),
                                        AX.X, ALU.add).then_inc(z0_ready, 1)

            def low_x0t(g, e):
                dve.wait_ge(x0t_hi_ready, g + 1)
                nc.vector.tensor_tensor(x0t_parts[:, :, 1], x0t[:, e], x0t_parts[:, :, 0].bitcast(f32),
                                        ALU.subtract).then_inc(x0t_lo_ready, 1)

            def add_chunk(g, e, s):
                i, (j, c) = VEC.index(s), divmod(s, NC)
                acc, y = sums[:, j % 2, 0], y_ps[s % YB]
                if c == 0:
                    dve.wait_ge(x2_summed, g * NT + j + FREE - 1)
                else:
                    dve.wait_ge(y_used_vec, g * NV + i + FREE)
                dve.wait_ge(y_made, g * NY + s + 1)
                if c == 0:
                    nc.vector.tensor_tensor(acc.rearrange("n (m o) -> n m o", m=MC),
                                            y[:, :].rearrange("n (m o) -> n m o", m=MC),
                                            x0t[:, e, j, 0:MC].unsqueeze(2).to_broadcast([128, MC, O]),
                                            ALU.mult).then_inc(y_used_vec, 1)
                    return
                for r in range(MC):
                    o, m = slice(r * O, (r + 1) * O), c * MC + r
                    ins = nc.vector.scalar_tensor_tensor(acc[:, o], y[:, o], x0t[:, e, j, m:m + 1], acc[:, o],
                                                         ALU.mult, ALU.add)
                ins.then_inc(y_used_vec, 1)

            def sum_tile(g, j):
                k = g * NT + j
                dve.wait_ge(y_used_vec, g * NV + VEC.index(slots_of("V", j)[-1]) + 1 + FREE)
                dve.wait_ge(y_used_sca, g * NS + SCA.index(slots_of("A", j)[-1]) + 1 + FREE)
                dve.wait_ge(terms_added, k * NA + NA)
                dve.wait_ge(x2_ready, k + FREE)
                nc.vector.tensor_reduce(x2[:, :], sums[:, j % 2, 0:NSUM].rearrange("n s (r o) -> n o (s r)", o=O),
                                        AX.X, ALU.add).then_inc(x2_summed, 1)

            def low_x2(g, j):
                k, p = g * NT + j, j % 2
                dve.wait_ge(x2_hi_ready, k + 1)
                nc.vector.tensor_tensor(x2_lo[:, p], x2[:, :], x2_hi[:, p].bitcast(f32),
                                        ALU.subtract).then_inc(x2_ready, 1)

            def group(g, e):
                more = not isinstance(g, int) or g < NG - 1
                dve.wait_ge(x0t_ready, g + 1)
                for s in VEC:
                    j, c = divmod(s, NC)
                    last_tile = (g, j - 1) if j > 0 else (g - 1, NT - 1)
                    add_chunk(g, e, s)
                    if c == SUM_AT and (j > 0 or after_first(g)):
                        sum_tile(*last_tile)
                    if c == LOW_AT and (j > 0 or after_first(g)):
                        low_x2(*last_tile)
                    if more and s in PAIR_SLOTS:
                        pair_products(g + 1, PAIR_SLOTS.index(s))
                    if more and s in LO_SLOTS:
                        low_pairs(g + 1, LO_SLOTS.index(s))
                    if more and s == X1_SLOTS_VEC[0]:
                        split_x1_tile(g + 1, 1 - e)
                    if more and s == X1_SLOTS_VEC[1]:
                        split_x1_rest(g + 1, 1 - e)
                if more:
                    low_x0t(g + 1, 1 - e)

            def pair(g, i, mlp=None):
                group(g, 0)
                group(g + 1, 1)

            for free in (y_used_vec, x2_summed, x2_ready):
                dve.sem_inc(free, FREE)
            dve.wait_ge(w0_loaded, 32)
            nc.vector.tensor_tensor(w0[:, :, :].rearrange("p c o -> p (c o)"),
                                    w0[:, :, :].rearrange("p c o -> p (c o)"), w0_raw, ALU.add).then_inc(w0_ready, 1)
            dve.wait_ge(w0_hi_ready, 1)
            nc.vector.tensor_tensor(w0_parts[:, 1], w0[:, SPLIT[0]:SPLIT[-1] + 1], w0_parts[:, 0].bitcast(f32),
                                    ALU.subtract).then_inc(w0_lo_ready, 1)
            dve.wait_ge(k1_hi_ready, 1)
            nc.vector.tensor_tensor(k1_lo[:, :], k1_raw, k1_hi[:, :].bitcast(f32), ALU.subtract
                                    ).then_inc(k1_lo_ready, 1)
            for c in range(NP):
                pair_products(0, c)
            for n in range(len(SPLIT)):
                low_pairs(0, n)
            split_x1_tile(0, 0)
            split_x1_rest(0, 0)
            dve.wait_ge(x0t_ready, 1)
            low_x0t(0, 0)
            all_pairs(dve, pair)
            sum_tile(NG - 1, NT - 1)
            low_x2(NG - 1, NT - 1)


def kernel(**inputs):
    import numpy as np
    import concourse.bacc as bacc
    from concourse.bass_utils import run_bass_kernel_spmd

    def host(name):
        return np.ascontiguousarray(inputs[name])

    k0 = host("L0_rec_k0")
    h = np.arange(M)
    k0_pairs = np.zeros((M, RC, NP, O), k0.dtype)
    k0_swapped = np.zeros((M, RC, NP, O), k0.dtype)
    for a in range(RC):
        for c in range(NP):
            r = RC * c + a
            m = (h + r) % M
            k0_pairs[:, a, c] = k0[:, h, m].T
            if 0 < r < M // 2:
                k0_swapped[:, a, c] = k0[:, m, h].T
    block_mask = np.repeat(np.eye(TB, dtype=np.float32), D, axis=0)

    starts = np.cumsum([0] + [inputs[f"tbl_{m}"].shape[0] for m in range(M - 1)]).astype(np.int32)

    w1 = host("W_top1")
    arrays = {
        "ids": host("ids").reshape(NG, GB, LP, LM).transpose(0, 2, 1, 3).reshape(NG, 128, LM),
        "table_starts": np.repeat(starts.reshape(LP, LM), GB, axis=0),
        "tables": np.concatenate([host(f"tbl_{m}") for m in range(M)]),
        "dense_t": host("dense_ctx").T,
        "k0_pairs": k0_pairs.reshape(PR, NP, O),
        "k0_swapped": k0_swapped.reshape(PR, NP, O),
        "k1_t": host("L0_rec_k1").transpose(1, 2, 0).reshape(O, M * O),
        "k2_t": host("L0_rec_k2").transpose(1, 2, 0),
        "w1_z": w1[:3 * O].reshape(3, O, H1).transpose(1, 0, 2),
        "w1_dense": w1[3 * O:],
        "b1": host("b_top1").reshape(H1 // 128, 128).T,
        "w2": host("W_top2").reshape(H1 // 128, 128, H2).transpose(1, 0, 2),
        "b2": host("b_top2").reshape(H2 // 128, 128).T,
        "w3": host("W_top3").reshape(H2 // 128, 128).T,
        "block_mask": block_mask,
        "identity": np.eye(M, dtype=np.float32),
    }
    arrays = {f"in_{k}": np.ascontiguousarray(v) for k, v in arrays.items()}

    nc = bacc.Bacc("TRN2", target_bir_lowering=False, num_devices=1)
    aps = {k[3:]: nc.dram_tensor(k, v.shape, mybir.dt.from_np(v.dtype), kind="ExternalInput").ap()
           for k, v in arrays.items()}
    out = nc.dram_tensor("out", (1, B), mybir.dt.float32, kind="ExternalOutput").ap()
    cin_tower(nc, out=out, **aps)
    result = run_bass_kernel_spmd(nc, [arrays], core_ids=[0])
    return result.results[0]["out"].reshape(B, 1)
```
